# Optimizing a Trainium2 kernel written in Bass

```python
import numpy as np
import jax
import jax.numpy as jnp

def _softmax(x, axis=-1):
    return jax.nn.softmax(x, axis=axis)

def _gelu(x):
    return jax.nn.gelu(x, approximate=True)

def _silu(x):
    return jax.nn.silu(x)

def _sigmoid(x):
    return jax.nn.sigmoid(x)

def _layernorm(x, axis=-1, eps=1e-05):
    m = jnp.mean(x, axis=axis, keepdims=True)
    v = jnp.var(x, axis=axis, keepdims=True)
    return (x - m) / jnp.sqrt(v + eps)

def _scatter_add(tgt, idx, src, axis=0):
    return tgt.at[idx].add(src)

def _segment_sum(src, seg, n):
    return jax.ops.segment_sum(src, seg, n)
kernel_name = 'mk_seq_postln_d1_jaxref_r8_ffadcc'

def setup_inputs(seed: int=0):
    np.random.seed(seed)
    _w = jnp.asarray

    def _L0_attn_setup():
        import jax, jax.numpy as jnp
        import numpy as np
        import math
        D = 128
        key = jax.random.key(seed)
        ks = jax.random.split(key, 5)
        B, S = (4, 256)
        scale = 1.0 / math.sqrt(D)
        x = jax.random.normal(ks[0], (B, S, D), dtype=jnp.float32)
        W_qkv = jax.random.normal(ks[1], (D, 3 * D), dtype=jnp.float32) * scale
        b_qkv = jax.random.normal(ks[2], (3 * D,), dtype=jnp.float32) * 0.01
        W_out = jax.random.normal(ks[3], (D, D), dtype=jnp.float32) * scale
        b_out = jax.random.normal(ks[4], (D,), dtype=jnp.float32) * 0.01
        return {'x': x, 'W_qkv': W_qkv, 'b_qkv': b_qkv, 'W_out': W_out, 'b_out': b_out}
    _L0_attn_in = _L0_attn_setup()

    def _L0_ffn_setup():
        import jax, jax.numpy as jnp
        import numpy as np
        HIDDEN = 128
        INTER = 512
        NUM_EXPERTS = 8
        TOP_K = 2
        EPS = 1e-05

        def _layer_norm(x, g, b):
            m = jnp.mean(x, axis=-1, keepdims=True)
            v = jnp.mean(jnp.square(x - m), axis=-1, keepdims=True)
            return (x - m) * jax.lax.rsqrt(v + EPS) * g + b
        key = jax.random.key(seed)
        ks = jax.random.split(key, 8)
        s = 0.02
        return {'x': jax.random.normal(ks[0], (4, 256, HIDDEN), dtype=jnp.float32), 'ln1_g': jnp.ones((HIDDEN,), jnp.float32), 'ln1_b': jnp.zeros((HIDDEN,), jnp.float32), 'attn_w': jax.random.normal(ks[1], (HIDDEN, HIDDEN), jnp.float32) * s, 'ln2_g': jnp.ones((HIDDEN,), jnp.float32), 'ln2_b': jnp.zeros((HIDDEN,), jnp.float32), 'gate_w': jax.random.normal(ks[2], (NUM_EXPERTS, HIDDEN), jnp.float32) * s, 'gate_proj': jax.random.normal(ks[3], (NUM_EXPERTS, INTER, HIDDEN), jnp.float32) * s, 'up_proj': jax.random.normal(ks[4], (NUM_EXPERTS, INTER, HIDDEN), jnp.float32) * s, 'down_proj': jax.random.normal(ks[5], (NUM_EXPERTS, HIDDEN, INTER), jnp.float32) * s}
    _L0_ffn_in = _L0_ffn_setup()
    _d = {'L0_attn_x': _L0_attn_in['x'], 'L0_attn_W_qkv': _L0_attn_in['W_qkv'], 'L0_attn_b_qkv': _L0_attn_in['b_qkv'], 'L0_attn_W_out': _L0_attn_in['W_out'], 'L0_attn_b_out': _L0_attn_in['b_out'], 'L0_ffn_ln1_g': _L0_ffn_in['ln1_g'], 'L0_ffn_ln1_b': _L0_ffn_in['ln1_b'], 'L0_ffn_attn_w': _L0_ffn_in['attn_w'], 'L0_ffn_ln2_g': _L0_ffn_in['ln2_g'], 'L0_ffn_ln2_b': _L0_ffn_in['ln2_b'], 'L0_ffn_gate_w': _L0_ffn_in['gate_w'], 'L0_ffn_gate_proj': _L0_ffn_in['gate_proj'], 'L0_ffn_up_proj': _L0_ffn_in['up_proj'], 'L0_ffn_down_proj': _L0_ffn_in['down_proj']}
    _x0 = _d['L0_attn_x']
    _d['L0_attn_x'] = jax.random.normal(jax.random.fold_in(jax.random.key(seed), 1), (16, 256, 128), dtype=_x0.dtype)
    del _x0
    return _d

def reference(L0_attn_x, L0_attn_W_qkv, L0_attn_b_qkv, L0_attn_W_out, L0_attn_b_out, L0_ffn_ln1_g, L0_ffn_ln1_b, L0_ffn_attn_w, L0_ffn_ln2_g, L0_ffn_ln2_b, L0_ffn_gate_w, L0_ffn_gate_proj, L0_ffn_up_proj, L0_ffn_down_proj):

    def _L0_attn_ref(x, W_qkv, b_qkv, W_out, b_out):
        import jax, jax.numpy as jnp
        import numpy as np
        import math
        D = 128
        qkv = x @ W_qkv + b_qkv
        q, k, v = jnp.split(qkv, 3, axis=-1)
        inv_sqrt_d = 1.0 / math.sqrt(D)
        scores = jnp.einsum('bqd,bkd->bqk', q, k) * inv_sqrt_d
        attn = jax.nn.softmax(scores, axis=-1)
        ctx = jnp.einsum('bqk,bkd->bqd', attn, v)
        return ctx @ W_out + b_out

    def _L0_ffn_ref(x, ln1_g, ln1_b, attn_w, ln2_g, ln2_b, gate_w, gate_proj, up_proj, down_proj):
        import jax, jax.numpy as jnp
        import numpy as np
        HIDDEN = 128
        INTER = 512
        NUM_EXPERTS = 8
        TOP_K = 2
        EPS = 1e-05

        def _layer_norm(x, g, b):
            m = jnp.mean(x, axis=-1, keepdims=True)
            v = jnp.mean(jnp.square(x - m), axis=-1, keepdims=True)
            return (x - m) * jax.lax.rsqrt(v + EPS) * g + b
        B, S, H = x.shape
        h = x + jnp.einsum('bsh,oh->bso', _layer_norm(x, ln1_g, ln1_b), attn_w)
        t = _layer_norm(h, ln2_g, ln2_b).reshape(-1, H)
        T = t.shape[0]
        logits = jnp.einsum('th,eh->te', t, gate_w)
        top_vals, top_idx = jax.lax.top_k(logits, TOP_K)
        rw = jax.nn.softmax(top_vals, axis=-1)
        comb = jnp.zeros((T, NUM_EXPERTS), dtype=t.dtype)
        comb = comb.at[jnp.arange(T)[:, None], top_idx].add(rw)
        out = jnp.zeros_like(t)
        for e in range(NUM_EXPERTS):
            g = jnp.einsum('th,ih->ti', t, gate_proj[e])
            u = jnp.einsum('th,ih->ti', t, up_proj[e])
            oe = jnp.einsum('ti,hi->th', jax.nn.silu(g) * u, down_proj[e])
            out = out + comb[:, e:e + 1] * oe
        return h + out.reshape(B, S, H)
    x = L0_attn_x
    x = _layernorm(x + _L0_attn_ref(x, L0_attn_W_qkv, L0_attn_b_qkv, L0_attn_W_out, L0_attn_b_out), axis=-1)
    x = _layernorm(x + _L0_ffn_ref(x, L0_ffn_ln1_g, L0_ffn_ln1_b, L0_ffn_attn_w, L0_ffn_ln2_g, L0_ffn_ln2_b, L0_ffn_gate_w, L0_ffn_gate_proj, L0_ffn_up_proj, L0_ffn_down_proj), axis=-1)
    return x

_drawn_inputs = setup_inputs


def setup_inputs(seed=0):
    import zlib

    import numpy as np

    out = dict(_drawn_inputs(seed))
    spreads = {'L0_ffn_ln1_g': (1.0, 0.6),
     'L0_ffn_ln1_b': (0.0, 0.681),
     'L0_ffn_ln2_g': (1.0, 0.6),
     'L0_ffn_ln2_b': (0.0, 0.8)}
    factors = {'L0_attn_b_qkv': 5.273,
     'L0_attn_b_out': 5.545,
     'L0_ffn_gate_w': 8.0,
     'L0_ffn_gate_proj': 8.0,
     'L0_ffn_up_proj': 8.0,
     'L0_ffn_down_proj': 8.0}
    for name, (base, spread) in spreads.items():
        noise = np.random.default_rng([zlib.crc32(name.encode()), seed]).standard_normal(out[name].shape)
        drawn = base * np.exp(spread * noise) if base else spread * noise
        out[name] = jnp.asarray(drawn.astype(out[name].dtype))
    for name, factor in factors.items():
        out[name] = (out[name] * factor).astype(out[name].dtype)
    return out
```

```python
import concourse.bass as bass
import concourse.mybir as mybir
from contextlib import ExitStack
import numpy as np

F32 = mybir.dt.float32
F32R = mybir.dt.float32r
BF16 = mybir.dt.bfloat16
I32 = mybir.dt.int32
U32 = mybir.dt.uint32
ALU = mybir.AluOpType
ACT = mybir.ActivationFunctionType
AX = mybir.AxisListType

B, S, D = 16, 256, 128
P = 128
NT = S // P
T = B * S
E, TOPK, INTER = 8, 2, 512
NC = INTER // P
EPS = 1e-5
QSCALE = float(D) ** -0.5
ROW = D + 2
REGION = T + P
PAD_ROW = E * REGION
X_ROWS = PAD_ROW + P
Y_ROWS = T * TOPK
MOE_TILES = T * TOPK // P + E - 1
TOKEN_TILES = T // P

WQ, WK, WVT, WO, AW, GW = 0, 128, 256, 384, 512, 640
BOUT = 648
BQ, BK, BV, G1, B1, G2, B2 = range(776, 783)
NPAR = 783
C_ID, C_TRI, C_ONE, C_IOTA8, C_BASE, C_TILE, C_CUM = 0, 128, 256, 384, 392, 400, 471
NCON = 471 + 64


def constants():
    c = np.zeros((P, NCON), np.float32)
    c[:, C_ID:C_ID + P] = np.eye(P)
    c[:, C_TRI:C_TRI + P] = np.triu(np.ones((P, P)), 1)
    c[:, C_ONE:C_ONE + P] = 1.0
    c[:, C_IOTA8:C_IOTA8 + E] = np.arange(E)
    c[:, C_BASE:C_BASE + E] = np.arange(E) * REGION
    c[:, C_TILE:C_TILE + MOE_TILES] = np.arange(MOE_TILES)
    c[:, C_CUM:C_CUM + E * E] = np.tril(np.ones((E, E))).reshape(-1)
    return c


def destinations():
    p = np.arange(P)[:, None, None]
    t = np.arange(TOKEN_TILES)[None, :, None]
    d = (p + P * t) * TOPK + np.arange(TOPK)[None, None, :]
    fill = Y_ROWS + np.arange(P)[:, None]
    return np.concatenate([d.reshape(P, -1), fill], axis=1).astype(np.int32)


NDST = TOKEN_TILES * TOPK + 1


def block_kernel(nc, x, par, con, dst, weights, out):
    x_v = x.rearrange("b (t p) d -> b p t d", p=P)
    w_v = weights.rearrange("p (j n) -> p j n", j=3)
    out_v = out.rearrange("b (t p) d -> b p t d", p=P)
    expert_rows = nc.dram_tensor("expert_rows", [X_ROWS, ROW], F32, kind="Internal").ap()
    moe_rows = nc.dram_tensor("moe_rows", [Y_ROWS, D], F32, kind="Internal").ap()
    moe_v = moe_rows.rearrange("(b t p k) d -> b p t (k d)", p=P, k=TOPK, t=NT)

    with ExitStack() as ctx:
        def sb(name, shape, dt=F32):
            return ctx.enter_context(nc.sbuf_tensor(name, shape, dt))

        def pair(name, shape, dt=F32):
            return [sb(f"{name}{i}", shape, dt) for i in range(2)]

        def sem(name):
            return ctx.enter_context(nc.semaphore(name))

        params = sb("params", [P, NPAR])
        const = sb("const", [P, NCON])
        dests = sb("dests", [P, NDST], I32)
        tri = sb("tri", [P, P], BF16)
        ones = sb("ones", [P, P], BF16)
        wvo = sb("wvo", [P, D])
        bq_s = sb("bq_s", [P, 1])
        bv_wide = sb("bv_wide", [P, P])
        bias_out = sb("bias_out", [P, NT, D])
        mhalf = sb("mhalf", [P, 2 * NT])
        res = sb("res", [P, B * S])
        xin = pair("xin", [P, NT, D])
        xT = pair("xT", [P, S])
        qT = pair("qT", [P, S])
        kT = pair("kT", [P, S])
        vo = pair("vo", [P, NT, D])
        prob = pair("prob", [P, NT, S])
        probT = pair("probT", [P, NT, S])
        n1 = pair("n1", [P, NT, D])
        n1T = pair("n1T", [P, S])
        x1 = pair("x1", [P, NT, D])
        h = pair("h", [P, NT, D])
        rows = pair("rows", [P, NT, TOPK, ROW])
        tT = pair("tT", [P, S])
        negmax = pair("negmax", [P, NT])
        rsum = pair("rsum", [P, NT])
        rinv = pair("rinv", [P, NT])
        st = sb("st", [P, NT, 6])
        mv0 = pair("mv0", [P, NT, 2])
        va = sb("va", [P, 2, NT])
        rs0 = pair("rs0", [P, 2, NT])
        st2 = sb("st2", [P, NT, 6])
        mv2 = pair("mv2", [P, NT, 2])
        vb = sb("vb", [P, NT])
        rs2 = pair("rs2", [P, NT])
        lg = sb("lg", [P, NT, E])
        top = pair("top", [P, NT, 8])
        topi = sb("topi", [P, NT, 8], U32)
        topf = sb("topf", [P, NT, TOPK])
        onehot = sb("onehot", [P, NT, TOPK, E])
        member = pair("member", [P, NT, E], BF16)
        base = sb("base", [P, E])
        slots = sb("slots", [P, NT, E])
        picked = sb("picked", [P, NT, TOPK, E])
        place = pair("place", [P, NT, TOPK], I32)
        gap = pair("gap", [P, NT])
        ex = pair("ex", [P, NT])
        exp1 = sb("exp1", [P, NT])
        wts = sb("wts", [P, NT, TOPK])
        cnt = sb("cnt", [1, E])
        cnt_i = sb("cnt_i", [1, E], I32)
        til_i = sb("til_i", [1, E], I32)
        til = sb("til", [1, E])
        cumm = sb("cumm", [1, E, E])
        cum = sb("cum", [1, E])
        done = sb("done", [1, MOE_TILES, E])
        donet = sb("donet", [1, MOE_TILES, E])
        eidx = sb("eidx", [1, MOE_TILES])
        past = sb("past", [1, MOE_TILES])
        row_f = sb("row_f", [1, MOE_TILES])
        ereg = sb("ereg", [1, MOE_TILES])
        woff = sb("woff", [1, MOE_TILES], I32)
        rowoff = sb("rowoff", [1, MOE_TILES], I32)
        fill_at = sb("fill_at", [1, E], I32)
        fill = sb("fill", [P, ROW])
        NW = E * INTER
        WP = NW // B
        w_raw = pair("w_raw", [P, 3, WP])
        wg_hi, wu_hi, wd_hi = (sb(f"w{n}_hi", [P, NW], F32R) for n in "gud")
        wg_lo, wu_lo, wd_lo = (sb(f"w{n}_lo", [P, NW], F32R) for n in "gud")
        xrow = pair("xrow", [P, ROW])
        t32 = sb("t32", [P, P])
        t_hi = pair("t_hi", [P, P], F32R)
        t_lo = pair("t_lo", [P, P], F32R)
        sg = pair("sg", [P, INTER])
        hid = pair("hid", [P, INTER])
        h_hi = pair("h_hi", [P, INTER], F32R)
        h_lo = pair("h_lo", [P, INTER], F32R)
        idx_a = pair("idx_a", [P, 1], I32)
        idx_b = pair("idx_b", [P, 1], I32)
        zero_i = sb("zero_i", [P, 1], I32)
        wt_a = pair("wt_a", [P, 1])
        ysb = pair("ysb", [P, D])
        NY = 4
        yin = [sb(f"yin{i}", [P, NT, TOPK, D]) for i in range(2)]
        z = pair("z", [P, NT, D])
        st3 = sb("st3", [P, NT, 6])
        mv3 = pair("mv3", [P, NT, 2])
        vc = sb("vc", [P, NT])
        rs3 = pair("rs3", [P, NT])
        osb = pair("osb", [P, NT, D])

        banks = [ctx.enter_context(nc.psum_tensor(f"bank{i}", [P, 512], F32)) for i in range(8)]
        ps_q, ps_v = banks[0][:, 0:256], banks[0][:, 256:512]
        ps_k = banks[1][:, 0:256]
        ps_s = banks[2][:, :]
        ps_p = banks[3][:, :]
        ps_o = banks[4][:, 0:256]
        ps_a = banks[5][:, 0:256]
        ps_n2 = ps_n1 = ps_x = banks[6][:, 0:256]
        ps_l = banks[7][:, 0:NT * E].rearrange("p (t e) -> p t e", t=NT)
        ps_r = banks[7][:, 64:64 + NT * E].rearrange("p (t e) -> p t e", t=NT)
        ps_t = banks[7][:, 128:128 + E]
        ident = const[:, C_ID:C_ID + P]

        names = ("par_in con_in dst_in cast_done wvo_done wvo_copied bias_ready bq_ready bv_ready half_ready "
                 "xb_done xT_ps xT_sb k_ps q_sb kk_sb v_ps v_sb s_ps max_done prob_done pT_ps pT_sb "
                 "o_ps rinv_done y_done st0_done mv0_done va_done rs0_done n1_done x1_done n1T_ps n1T_sb "
                 "a_ps h_done st2_done mv2_done vb_done rs2_done n2_done n2T_ps tT_sb l_ps lg_done "
                 "top_done topi_done topf_done onehot_done member_done gap_done ex_done exp1_done wts_done meta_done "
                 "t_ps slots_done picked_done place_done base_done base_init res_done "
                 "cnt_done cnti_done tili_done til_done cumm_done cum_done dn_done dnt_done eidx_done past_done ereg_done row_done "
                 "plan_done fill_ready fill_done w_hi w_lo "
                 "xr_ps t32_done thi_done tlo_done g_ps u_ps sg_done hid_done hT_ps hhi_done hlo_done y_ps ysb_done "
                 "zero_ready idxa_done idxb_done wta_done "
                 "z0_done z_done st3_done mv3_done vc_done rs3_done o_done").split()
        sm = {n: sem(n) for n in names}
        x_in = [sem(f"x_in{i}") for i in range(2)]
        w_in = [sem(f"w_in{i}") for i in range(2)]
        sent = [sem(f"sent{i}") for i in range(2)]
        xr_in = [sem(f"xr_in{i}") for i in range(2)]
        y_sent = [sem(f"y_sent{i}") for i in range(2)]
        y_in = [sem(f"y_in{i}") for i in range(2)]
        o_sent = [sem(f"o_sent{i}") for i in range(2)]

        block = ctx.enter_context(nc.Block())

        def straight_steps(step, n_items, depth):
            for s in range(n_items + depth):
                step(s, s % 2, lambda lag, s=s: 0 <= s - lag < n_items)

        def run_steps(eng, step, n_items, depth):
            first = depth + depth % 2 + 2
            pairs = (n_items - first) // 2
            for s in range(first):
                step(s, s % 2, lambda lag, s=s: 0 <= s - lag < n_items)
            with eng.Fori(0, pairs) as i:
                for half in range(2):
                    step(i * 2 + (first + half), half, lambda lag: True)
            for s in range(first + 2 * pairs, n_items + depth):
                step(s, s % 2, lambda lag, s=s: 0 <= s - lag < n_items)

        LAST = 4

        def resid(b):
            return res[:, bass.ds(b * S, S)]

        def resid_v(b):
            return resid(b).rearrange("p (t d) -> p t d", t=NT)

        def resid_t(b, t):
            return res[:, bass.ds(b * S + t * P, P)]

        @block.sync
        def _(sp):
            sp.dma_start(params[:, :], par).then_inc(sm["par_in"], 16)
            sp.dma_start(const[:, :], con).then_inc(sm["con_in"], 16)
            sp.dma_start(dests[:, :], dst).then_inc(sm["dst_in"], 16)

            def load_w(s, p_):
                if not isinstance(s, int) or s >= 2:
                    sp.wait_ge(sm["w_lo"], s - 1)
                sp.dma_start(w_raw[p_][:, :, :], w_v[:, :, bass.ds(s * WP, WP)]).then_inc(w_in[p_], 16)

            def front(s, par_, live):
                if live(0):
                    if not isinstance(s, int) or s >= 2:
                        sp.wait_ge(sm["xT_ps"], s - 1)
                        sp.wait_ge(sm["xb_done"], s - 1)
                    sp.dma_start(xin[par_][:, :, :], x_v[s if isinstance(s, int) else bass.ds(s, 1)]
                                 if isinstance(s, int) else
                                 x_v[bass.ds(s, 1), :, :, :].rearrange("a p t d -> p (a t) d")
                                 ).then_inc(x_in[par_], 16)
                    load_w(s, par_)

            straight_steps(front, B, 0)

            sp.wait_ge(sm["fill_ready"], 3)
            sp.dma_start(expert_rows[PAD_ROW:PAD_ROW + P, :], fill[:, :]).then_inc(sm["fill_done"], 16)
            for half in range(2):
                sp.wait_ge(sent[half], 16 * NT * TOPK * (B // 2))
            sp.wait_ge(sm["plan_done"], 3)
            for e in range(E):
                at = sp.value_load(fill_at[0:1, e:e + 1], min_val=0, max_val=X_ROWS - P)
                sp.dma_start(expert_rows[bass.ds(at, P), :], fill[:, :]).then_inc(sm["fill_done"], 16)
            sp.wait_ge(sm["fill_done"], 16 * (E + 1))

            def load_rows(s, p_, live):
                if live(0):
                    if not isinstance(s, int) or s >= 2:
                        sp.wait_ge(sm["xr_ps"], s - 1)
                        sp.wait_ge(sm["idxa_done"], s - 1)
                        sp.wait_ge(sm["wta_done"], s - 1)
                    at = sp.value_load(rowoff[0:1, bass.ds(s, 1)], min_val=0, max_val=X_ROWS - P)
                    sp.dma_start(xrow[p_][:, :], expert_rows[bass.ds(at, P), :]).then_inc(xr_in[p_], 16)

            run_steps(sp, load_rows, MOE_TILES, 0)

            sp.wait_ge(y_sent[0], 16 * ((MOE_TILES + 1) // 2))
            sp.wait_ge(y_sent[1], 16 * (MOE_TILES // 2))

            def load_moe(s, p_, live):
                if live(0):
                    if not isinstance(s, int) or s >= 2:
                        sp.wait_ge(sm["z_done"], s - 1)
                    src = (moe_v[s] if isinstance(s, int) else
                           moe_v[bass.ds(s, 1), :, :, :].rearrange("a p t d -> p (a t) d"))
                    sp.dma_start(yin[p_][:, :, :, :].rearrange("p t k d -> p t (k d)"), src
                                 ).then_inc(y_in[p_], 16)

            straight_steps(load_moe, B, 0)

        @block.tensor
        def _(pe):
            mm = nc.tensor.matmul
            pe.wait_ge(sm["par_in"], 16)
            pe.wait_ge(sm["con_in"], 16)
            mm(ps_o[:, 0:D], params[:, WVT:WVT + D], params[:, WO:WO + D], start=True, stop=True
               ).then_inc(sm["wvo_done"], 1)
            pe.wait_ge(sm["bv_ready"], 1)
            mm(ps_a[:, 0:D], bv_wide[:, :], params[:, WO:WO + D], start=True, stop=True
               ).then_inc(sm["wvo_done"], 1)
            pe.wait_ge(sm["cast_done"], 2)

            def front(s, p, live):
                q = 1 - p
                if live(1):
                    b = s - 1
                    pe.wait_ge(sm["xT_sb"], b + 1)
                    if not isinstance(s, int) or b >= 1:
                        pe.wait_ge(sm["kk_sb"], b)
                        pe.wait_ge(sm["v_sb"], b)
                    mm(ps_k, params[:, WK:WK + D], xT[q][:, :], start=True, stop=True).then_inc(sm["k_ps"], 1)
                    mm(ps_q, params[:, WQ:WQ + D], xT[q][:, :], start=True, stop=True)
                    if isinstance(s, int) and b == 0:
                        pe.wait_ge(sm["wvo_copied"], 1)
                    for t in range(NT):
                        mm(ps_v[:, t * P:(t + 1) * P], xT[q][:, t * P:(t + 1) * P], wvo[:, :],
                           start=True, stop=True).then_inc(sm["v_ps"], 1)
                if live(4):
                    b = s - 4
                    pe.wait_ge(sm["n2_done"], NT * b + NT)
                    pe.wait_ge(sm["xT_sb"], min(s, B))
                    for t in range(NT):
                        nc.tensor.transpose(ps_n2[:, t * P:(t + 1) * P], rows[p][:, t, 0, 0:D], ident
                                            ).then_inc(sm["n2T_ps"], 1)
                if live(2):
                    b = s - 2
                    pe.wait_ge(sm["prob_done"], NT * b + NT)
                    if not isinstance(s, int) or b >= 1:
                        pe.wait_ge(sm["pT_sb"], b)
                    for kt in range(NT):
                        for t in range(NT):
                            nc.tensor.transpose(ps_p[:, kt * S + t * P:kt * S + (t + 1) * P],
                                                prob[p][:, t, kt * P:(kt + 1) * P], ident
                                                ).then_inc(sm["pT_ps"], 1)
                if live(4):
                    b = s - 4
                    pe.wait_ge(sm["tT_sb"], b + 1)
                    if not isinstance(s, int) or b >= 1:
                        pe.wait_ge(sm["slots_done"], b)
                        pe.wait_ge(sm["base_done"], b)
                    for t in range(NT):
                        mm(ps_l[:, t, :], tT[p][:, t * P:(t + 1) * P], params[:, GW:GW + E],
                           start=True, stop=True).then_inc(sm["l_ps"], 1)
                if live(3):
                    b = s - 3
                    pe.wait_ge(sm["n1_done"], NT * b + NT)
                    pe.wait_ge(sm["tT_sb"] if live(4) else sm["xT_sb"], b if live(4) else min(s, B))
                    for t in range(NT):
                        nc.tensor.transpose(ps_n1[:, t * P:(t + 1) * P], n1[q][:, t, :], ident
                                            ).then_inc(sm["n1T_ps"], 1)
                if live(1):
                    b = s - 1
                    pe.wait_ge(sm["q_sb"], b + 1)
                    pe.wait_ge(sm["kk_sb"], b + 1)
                    if not isinstance(s, int) or b >= 1:
                        pe.wait_ge(sm["prob_done"], NT * b)
                    for t in range(NT):
                        mm(ps_s[:, t * S:(t + 1) * S], qT[q][:, t * P:(t + 1) * P], kT[q][:, :],
                           start=True, stop=True).then_inc(sm["s_ps"], 1)
                if live(0):
                    pe.wait_ge(x_in[p], (s // 2) * 16 + 16 if isinstance(s, int) else (s - p) * 8 + 16)
                    if live(3):
                        pe.wait_ge(sm["n1T_sb"], s - 2)
                    elif s >= 1:
                        pe.wait_ge(sm["xT_sb"], s)
                    for t in range(NT):
                        last = nc.tensor.transpose(ps_x[:, t * P:(t + 1) * P], xin[p][:, t, :], ident)
                    last.then_inc(sm["xT_ps"], 1)
                if live(4):
                    b = s - 4
                    pe.wait_ge(sm["member_done"], b + 1)
                    for t in range(NT):
                        for u in range(t):
                            mm(ps_r[:, t, :], ones[:, :], member[p][:, u, :], start=(u == 0), stop=False)
                        mm(ps_r[:, t, :], tri[:, :], member[p][:, t, :], start=(t == 0), stop=True)
                    for t in range(NT):
                        last = mm(ps_t, ones[:, :], member[p][:, t, :], start=(t == 0), stop=(t == NT - 1))
                    last.then_inc(sm["t_ps"], 1)
                if live(2):
                    b = s - 2
                    pe.wait_ge(sm["pT_sb"], b + 1)
                    pe.wait_ge(sm["v_sb"], b + 1)
                    if not isinstance(s, int) or b >= 1:
                        pe.wait_ge(sm["y_done"], NT * b)
                    else:
                        pe.wait_ge(sm["wvo_copied"], 1)
                    for t in range(NT):
                        for kt in range(NT):
                            last = mm(ps_o[:, t * P:(t + 1) * P], probT[p][:, kt, t * P:(t + 1) * P],
                                      vo[p][:, kt, :], start=(kt == 0), stop=(kt == NT - 1))
                        last.then_inc(sm["o_ps"], 1)
                if live(3):
                    b = s - 3
                    pe.wait_ge(sm["n1T_sb"], b + 1)
                    if not isinstance(s, int) or b >= 1:
                        pe.wait_ge(sm["h_done"], b)
                    else:
                        pe.wait_ge(sm["bias_ready"], 1)
                    for t in range(NT):
                        mm(ps_a[:, t * P:(t + 1) * P], n1T[q][:, t * P:(t + 1) * P],
                           params[:, AW:AW + D], start=True, stop=True).then_inc(sm["a_ps"], 1)

            straight_steps(front, B, LAST)

            pe.wait_ge(sm["w_lo"], B)
            pe.wait_ge(sm["base_done"], B)
            pe.wait_ge(sm["slots_done"], B)
            pe.wait_ge(sm["h_done"], B)
            pe.wait_ge(sm["tT_sb"], B)
            pe.wait_ge(sm["lg_done"], B)
            pe.wait_ge(sm["plan_done"], 3)

            def three(out_, st_hi, st_lo, mv_hi, mv_lo, first, last):
                mm(out_, st_hi, mv_hi, start=first, stop=False)
                mm(out_, st_hi, mv_lo, start=False, stop=False)
                return mm(out_, st_lo, mv_hi, start=False, stop=last)

            def experts(s, p, live):
                q = 1 - p
                if live(1):
                    i = s - 1
                    pe.wait_ge(sm["tlo_done"], i + 1)
                    if not isinstance(s, int) or i >= 2:
                        pe.wait_ge(sm["sg_done"], i - 1)
                        pe.wait_ge(sm["hid_done"], i - 1)
                    w = pe.value_load(woff[0:1, bass.ds(i, 1)], min_val=0, max_val=(E - 1) * INTER)
                    ws = bass.ds(w, INTER)
                    three(banks[q][:, :], t_hi[q][:, :], t_lo[q][:, :], wg_hi[:, ws], wg_lo[:, ws],
                          True, True).then_inc(sm["g_ps"], 1)
                    three(banks[2 + q][:, :], t_hi[q][:, :], t_lo[q][:, :], wu_hi[:, ws], wu_lo[:, ws],
                          True, True).then_inc(sm["u_ps"], 1)
                if live(0):
                    pe.wait_ge(xr_in[p], (s // 2) * 16 + 16 if isinstance(s, int) else (s - p) * 8 + 16)
                    if not isinstance(s, int) or s >= 1:
                        pe.wait_ge(sm["t32_done"], s)
                    nc.tensor.transpose(banks[6][:, 0:P], xrow[p][:, 0:D], ident
                                        ).then_inc(sm["xr_ps"], 1)
                if live(2):
                    i = s - 2
                    pe.wait_ge(sm["hid_done"], i + 1)
                    if not isinstance(s, int) or i >= 2:
                        pe.wait_ge(sm["hlo_done"], i - 1)
                        pe.wait_ge(sm["hhi_done"], i - 1)
                    for c in range(NC):
                        last = nc.tensor.transpose(banks[4 + p][:, c * P:(c + 1) * P],
                                                   hid[p][:, c * P:(c + 1) * P], ident)
                    last.then_inc(sm["hT_ps"], 1)
                if live(3):
                    i = s - 3
                    pe.wait_ge(sm["hlo_done"], i + 1)
                    if not isinstance(s, int) or i >= 1:
                        pe.wait_ge(sm["ysb_done"], i)
                    w = pe.value_load(woff[0:1, bass.ds(i, 1)], min_val=0, max_val=(E - 1) * INTER)
                    for c in range(NC):
                        ws = bass.ds(w + c * P, P)
                        cs = slice(c * P, (c + 1) * P)
                        last = three(banks[7][:, 0:P], h_hi[q][:, cs], h_lo[q][:, cs],
                                     wd_hi[:, ws], wd_lo[:, ws], c == 0, c == NC - 1)
                    last.then_inc(sm["y_ps"], 1)

            run_steps(pe, experts, MOE_TILES, 3)

        @block.scalar
        def _(act):
            A = nc.scalar.activation
            col = lambda c: params[:, c:c + 1]
            act.wait_ge(sm["par_in"], 16)
            nc.scalar.mul(bq_s[:, :], col(BQ), QSCALE).then_inc(sm["bq_ready"], 1)
            act.wait_ge(sm["con_in"], 16)
            act.wait_ge(sm["wvo_done"], 1)
            A(wvo[:, :], ps_o[:, 0:D], ACT.Copy).then_inc(sm["wvo_copied"], 1)
            act.wait_ge(sm["bq_ready"], 1)

            def front(s, p, live):
                q = 1 - p
                if live(1):
                    b = s - 1
                    act.wait_ge(sm["v_ps"], NT * b + NT)
                    if not isinstance(s, int) or b >= 2:
                        act.wait_ge(sm["s_ps"], NT * (b - 1))
                    A(qT[q][:, :], ps_q, ACT.Identity, bias=bq_s[:, :], scale=QSCALE).then_inc(sm["q_sb"], 1)
                    if not isinstance(s, int) or b >= 2:
                        act.wait_ge(sm["o_ps"], NT * (b - 1))
                    A(vo[q][:, :, :].rearrange("p t d -> p (t d)"), ps_v, ACT.Copy).then_inc(sm["v_sb"], 1)
                if live(4):
                    b = s - 4
                    act.wait_ge(sm["n2T_ps"], NT * b + NT)
                    if not isinstance(s, int) or b >= 2:
                        act.wait_ge(sm["l_ps"], NT * (b - 1))
                    A(tT[p][:, :], ps_n2, ACT.Identity, bias=col(B2), scale=col(G2)).then_inc(sm["tT_sb"], 1)
                if live(2):
                    b = s - 2
                    act.wait_ge(sm["pT_ps"], NT * NT * (b + 1))
                    if not isinstance(s, int) or b >= 2:
                        act.wait_ge(sm["o_ps"], NT * (b - 1))
                    A(probT[p][:, :, :].rearrange("p t d -> p (t d)"), ps_p, ACT.Copy).then_inc(sm["pT_sb"], 1)
                if live(3):
                    b = s - 3
                    act.wait_ge(sm["n1T_ps"], NT * b + NT)
                    if not isinstance(s, int) or b >= 2:
                        act.wait_ge(sm["a_ps"], NT * (b - 1))
                    A(n1T[q][:, :], ps_n1, ACT.Identity, bias=col(B1), scale=col(G1)).then_inc(sm["n1T_sb"], 1)
                if live(0):
                    act.wait_ge(sm["xT_ps"], s + 1)
                    if not isinstance(s, int) or s >= 2:
                        act.wait_ge(sm["v_ps"], NT * (s - 1))
                    A(xT[p][:, :], ps_x, ACT.Copy).then_inc(sm["xT_sb"], 1)
                if live(1):
                    b = s - 1
                    act.wait_ge(sm["max_done"], b + 1)
                    if not isinstance(s, int) or b >= 2:
                        act.wait_ge(sm["pT_ps"], NT * NT * (b - 1))
                        act.wait_ge(sm["rinv_done"], b - 1)
                    for t in range(NT):
                        A(prob[q][:, t, :], ps_s[:, t * S:(t + 1) * S], ACT.Exp, bias=negmax[q][:, t:t + 1],
                          accum_out=rsum[q][:, t:t + 1]).then_inc(sm["prob_done"], 1)
                if live(4):
                    b = s - 4
                    act.wait_ge(sm["gap_done"], b + 1)
                    if not isinstance(s, int) or b >= 2:
                        act.wait_ge(sm["wts_done"], 2 * (b - 1))
                    A(ex[p][:, :], gap[p][:, :], ACT.Exp).then_inc(sm["ex_done"], 1)

            straight_steps(front, B, LAST)

            def experts(s, p, live):
                q = 1 - p
                if live(1):
                    i = s - 1
                    act.wait_ge(sm["g_ps"], i + 1)
                    if not isinstance(s, int) or i >= 2:
                        act.wait_ge(sm["hid_done"], i - 1)
                    A(sg[q][:, :], banks[q][:, :], ACT.Silu).then_inc(sm["sg_done"], 1)
                if live(0):
                    act.wait_ge(sm["xr_ps"], s + 1)
                    if not isinstance(s, int) or s >= 1:
                        act.wait_ge(sm["tlo_done"], s)
                    A(t32[:, :], banks[6][:, 0:P], ACT.Identity, bias=col(B2),
                      scale=col(G2)).then_inc(sm["t32_done"], 1)
                if live(2):
                    i = s - 2
                    act.wait_ge(sm["hT_ps"], i + 1)
                    if not isinstance(s, int) or i >= 2:
                        act.wait_ge(sm["y_ps"], i - 1)
                    A(h_hi[p][:, :], banks[4 + p][:, :], ACT.Copy).then_inc(sm["hhi_done"], 1)
                if live(3):
                    i = s - 3
                    act.wait_ge(sm["y_ps"], i + 1)
                    if not isinstance(s, int) or i >= 2:
                        act.wait_ge(y_sent[q], ((i // 2) * 16) if isinstance(i, int) else (i - q) * 8)
                    A(ysb[q][:, :], banks[7][:, 0:P], ACT.Copy).then_inc(sm["ysb_done"], 1)

            run_steps(act, experts, MOE_TILES, 3)

            def finish(s, p, live):
                if live(1):
                    b, q = s - 1, 1 - p
                    act.wait_ge(sm["o_done"], NT * b + NT)
                    dst_ = (out_v[b] if isinstance(b, int) else
                            out_v[bass.ds(b, 1), :, :, :].rearrange("a p t d -> p (a t) d"))
                    act.dma_start(dst_, osb[q][:, :, :]).then_inc(o_sent[q], 16)

            straight_steps(finish, B, 1)
            for half in range(2):
                act.wait_ge(o_sent[half], 16 * (B // 2))

        @block.vector
        def _(dve):
            V = nc.vector
            dve.wait_ge(sm["par_in"], 16)
            V.tensor_copy(bv_wide[:, :], params[:, BV:BV + 1].to_broadcast([P, P])).then_inc(sm["bv_ready"], 1)
            V.memset(mhalf[:, :], -0.5).then_inc(sm["half_ready"], 1)
            dve.wait_ge(sm["con_in"], 16)
            V.tensor_copy(tri[:, :], const[:, C_TRI:C_TRI + P]).then_inc(sm["cast_done"], 1)
            V.tensor_copy(ones[:, :], const[:, C_ONE:C_ONE + P]).then_inc(sm["cast_done"], 1)
            V.tensor_copy(base[:, :], const[:, C_BASE:C_BASE + E]).then_inc(sm["base_init"], 1)
            dve.wait_ge(sm["wvo_done"], 2)
            V.tensor_tensor(bias_out[:, :, :], ps_a[:, 0:D].unsqueeze(1).to_broadcast([P, NT, D]),
                            params[:, BOUT:BOUT + D].unsqueeze(1).to_broadcast([P, NT, D]),
                            ALU.add).then_inc(sm["bias_ready"], 1)
            dve.wait_ge(sm["dst_in"], 16)
            V.memset(fill[:, 0:ROW], 0.0).then_inc(sm["fill_ready"], 1)
            dve.wait_ge(sm["fill_ready"], 1)
            V.tensor_copy(fill[:, D + 1:D + 2].bitcast(I32), dests[:, NDST - 1:NDST]).then_inc(sm["fill_ready"], 2)

            def split(s, p):
                dve.wait_ge(w_in[p], (s // 2) * 16 + 16 if isinstance(s, int) else (s - p) * 8 + 16)
                for j, hi in enumerate((wg_hi, wu_hi, wd_hi)):
                    V.tensor_copy(hi[:, bass.ds(s * WP, WP)], w_raw[p][:, j, :]).then_inc(sm["w_hi"], 1)

            def front(s, p, live):
                q = 1 - p
                if live(1):
                    b = s - 1
                    dve.wait_ge(sm["k_ps"], b + 1)
                    if not isinstance(s, int) or b >= 2:
                        dve.wait_ge(sm["s_ps"], NT * (b - 1))
                    V.tensor_scalar(kT[q][:, :], ps_k, params[:, BK:BK + 1], None, ALU.add).then_inc(sm["kk_sb"], 1)
                if live(4):
                    b = s - 4
                    dve.wait_ge(sm["l_ps"], NT * b + NT)
                    V.tensor_copy(lg[:, :, :], ps_l).then_inc(sm["lg_done"], 1)
                    dve.wait_ge(sm["lg_done"], b + 1)
                    if not isinstance(s, int) or b >= 2:
                        dve.wait_ge(sm["gap_done"], b - 1)
                    for t in range(NT):
                        V.max(top[p][:, t, :], lg[:, t, :]).then_inc(sm["top_done"], 1)
                    for t in range(NT):
                        dve.wait_ge(sm["top_done"], NT * b + t + 1)
                        V.max_index(topi[:, t, :], top[p][:, t, :], lg[:, t, :]).then_inc(sm["topi_done"], 1)
                    if not isinstance(s, int) or b >= 2:
                        dve.wait_ge(sm["ex_done"], b - 1)
                    V.tensor_tensor(gap[p][:, :], top[p][:, :, 1], top[p][:, :, 0], ALU.subtract
                                    ).then_inc(sm["gap_done"], 1)
                    dve.wait_ge(sm["topi_done"], NT * b + NT)
                    V.tensor_copy(topf[:, :, :], topi[:, :, 0:TOPK]).then_inc(sm["topf_done"], 1)
                    dve.wait_ge(sm["topf_done"], b + 1)
                    if not isinstance(s, int) or b >= 1:
                        dve.wait_ge(sm["picked_done"], b)
                    V.tensor_tensor(onehot[:, :, :, :].rearrange("p t k e -> p (t k) e"),
                                    topf[:, :, :].rearrange("p t k -> p (t k)").unsqueeze(2).to_broadcast([P, NT * TOPK, E]),
                                    const[:, C_IOTA8:C_IOTA8 + E].unsqueeze(1).to_broadcast([P, NT * TOPK, E]),
                                    ALU.is_equal).then_inc(sm["onehot_done"], 1)
                    dve.wait_ge(sm["onehot_done"], b + 1)
                    if not isinstance(s, int) or b >= 2:
                        dve.wait_ge(sm["t_ps"], b - 1)
                    V.tensor_tensor(member[p][:, :, :], onehot[:, :, 0, :], onehot[:, :, 1, :], ALU.add
                                    ).then_inc(sm["member_done"], 1)
                if live(1):
                    b = s - 1
                    dve.wait_ge(sm["s_ps"], NT * b + NT)
                    if not isinstance(s, int) or b >= 2:
                        dve.wait_ge(sm["prob_done"], NT * (b - 1))
                    V.tensor_reduce(negmax[q][:, :], ps_s.rearrange("p (t k) -> p t k", t=NT), AX.X, ALU.max,
                                    negate=True).then_inc(sm["max_done"], 1)
                if live(3):
                    b = s - 3
                    if not isinstance(s, int) or b >= 2:
                        dve.wait_ge(sm["res_done"], b - 1)
                    for t in range(NT):
                        V.tensor_scalar(x1[q][:, t, :], resid_t(b, t), mv0[q][:, t, 0:1], rs0[q][:, 0, t:t + 1],
                                        ALU.subtract, ALU.mult).then_inc(sm["x1_done"], 1)
                if live(4):
                    b = s - 4
                    dve.wait_ge(sm["t_ps"], b + 1)
                    if isinstance(s, int) and b == 0:
                        dve.wait_ge(sm["base_init"], 1)
                    else:
                        dve.wait_ge(sm["base_done"], b)
                    V.tensor_tensor(slots[:, :, :], ps_r, base[:, :].unsqueeze(1).to_broadcast([P, NT, E]),
                                    ALU.add).then_inc(sm["slots_done"], 1)
                    dve.wait_ge(sm["slots_done"], b + 1)
                    V.tensor_tensor(picked[:, :, :, :], onehot[:, :, :, :],
                                    slots[:, :, :].unsqueeze(2).to_broadcast([P, NT, TOPK, E]), ALU.mult
                                    ).then_inc(sm["picked_done"], 1)
                    V.tensor_tensor(base[:, :], ps_t, base[:, :], ALU.add).then_inc(sm["base_done"], 1)
                    dve.wait_ge(sm["ex_done"], b + 1)
                    V.tensor_scalar(exp1[:, :], ex[p][:, :], 1.0, None, ALU.add).then_inc(sm["exp1_done"], 1)
                    if not isinstance(s, int) or b >= 2:
                        dve.wait_ge(sent[p], ((b // 2) if isinstance(b, int) else (b - p)) *
                                    (16 * NT * TOPK if isinstance(b, int) else 8 * NT * TOPK))
                    dve.wait_ge(sm["picked_done"], b + 1)
                    with nc.allow_low_precision(reason="whole numbers below 2**24"):
                        V.tensor_reduce(place[p][:, :, :], picked[:, :, :, :], AX.X, ALU.add
                                        ).then_inc(sm["place_done"], 1)
                    dve.wait_ge(sm["exp1_done"], b + 1)
                    if not isinstance(s, int) or b >= 1:
                        dve.wait_ge(sm["meta_done"], 2 * b)
                    V.reciprocal(wts[:, :, 0], exp1[:, :]).then_inc(sm["wts_done"], 1)
                    dve.wait_ge(sm["wts_done"], 2 * b + 1)
                    V.tensor_tensor(wts[:, :, 1], wts[:, :, 0], ex[p][:, :], ALU.mult).then_inc(sm["wts_done"], 1)
                    V.tensor_copy(rows[p][:, :, :, D + 1].bitcast(I32),
                                  dests[:, bass.ds(b * (NT * TOPK), NT * TOPK)].rearrange("p (t k) -> p t k", t=NT)
                                  ).then_inc(sm["meta_done"], 1)
                    dve.wait_ge(sm["wts_done"], 2 * b + 2)
                    V.tensor_copy(rows[p][:, :, :, D], wts[:, :, :]).then_inc(sm["meta_done"], 1)
                if live(2):
                    b = s - 2
                    dve.wait_ge(sm["prob_done"], NT * b + NT)
                    V.reciprocal(rinv[p][:, :], rsum[p][:, :]).then_inc(sm["rinv_done"], 1)
                    dve.wait_ge(sm["rinv_done"], b + 1)
                    dve.wait_ge(sm["xb_done"], b + 1)
                    dve.wait_ge(sm["o_ps"], NT * b + NT)
                    for t in range(NT):
                        V.scalar_tensor_tensor(resid_t(b, t), ps_o[:, t * P:(t + 1) * P], rinv[p][:, t:t + 1],
                                               resid_t(b, t), ALU.mult, ALU.add).then_inc(sm["y_done"], 1)
                    for t in range(NT):
                        dve.wait_ge(sm["y_done"], NT * b + t + 1)
                        if not isinstance(s, int) or b >= 1:
                            dve.wait_ge(sm["mv0_done"], NT * b)
                        V.bn_stats(st[:, t, :], resid_t(b, t)).then_inc(sm["st0_done"], 1)
                    for t in range(NT):
                        dve.wait_ge(sm["st0_done"], NT * b + t + 1)
                        if not isinstance(s, int) or b >= 2:
                            dve.wait_ge(sm["va_done"], 2 * (b - 1))
                        V.bn_aggr(mv0[p][:, t, :], st[:, t, :]).then_inc(sm["mv0_done"], 1)
                if live(3):
                    b = s - 3
                    dve.wait_ge(sm["a_ps"], NT * b + NT)
                    dve.wait_ge(sm["x1_done"], NT * b + NT)
                    if not isinstance(s, int) or b >= 2:
                        dve.wait_ge(sm["res_done"], b - 1)
                    V.tensor_tensor(h[q][:, :, :].rearrange("p t d -> p (t d)"), ps_a,
                                    x1[q][:, :, :].rearrange("p t d -> p (t d)"), ALU.add).then_inc(sm["h_done"], 1)
                    dve.wait_ge(sm["h_done"], b + 1)
                    if not isinstance(s, int) or b >= 1:
                        dve.wait_ge(sm["mv2_done"], NT * b)
                    for t in range(NT):
                        V.bn_stats(st2[:, t, :], h[q][:, t, :]).then_inc(sm["st2_done"], 1)
                    for t in range(NT):
                        dve.wait_ge(sm["st2_done"], NT * b + t + 1)
                        if not isinstance(s, int) or b >= 2:
                            dve.wait_ge(sm["vb_done"], b - 1)
                        V.bn_aggr(mv2[q][:, t, :], st2[:, t, :]).then_inc(sm["mv2_done"], 1)
                if live(2):
                    b = s - 2
                    dve.wait_ge(sm["rs0_done"], b + 1)
                    if not isinstance(s, int) or b >= 2:
                        dve.wait_ge(sm["n1T_ps"], NT * (b - 1))
                    for t in range(NT):
                        V.tensor_scalar(n1[p][:, t, :], resid_t(b, t), mv0[p][:, t, 0:1], rs0[p][:, 1, t:t + 1],
                                        ALU.subtract, ALU.mult).then_inc(sm["n1_done"], 1)
                if live(3):
                    b = s - 3
                    dve.wait_ge(sm["rs2_done"], b + 1)
                    if not isinstance(s, int) or b >= 2:
                        c = b // 2 if isinstance(b, int) else b - q
                        dve.wait_ge(sent[q], c * (16 * NT * TOPK if isinstance(b, int) else 8 * NT * TOPK))
                    for t in range(NT):
                        V.tensor_scalar(rows[q][:, t, :, 0:D], h[q][:, t, :].unsqueeze(1).to_broadcast([P, TOPK, D]),
                                        mv2[q][:, t, 0:1], rs2[q][:, t:t + 1],
                                        ALU.subtract, ALU.mult).then_inc(sm["n2_done"], 1)
                if live(0):
                    split(s, p)

            straight_steps(front, B, LAST)

            dve.wait_ge(sm["base_done"], B)
            V.tensor_tensor(cnt[:, :], base[0:1, :], const[0:1, C_BASE:C_BASE + E], ALU.subtract
                            ).then_inc(sm["cnt_done"], 1)
            V.tensor_copy(fill_at[:, :], base[0:1, :]).then_inc(sm["plan_done"], 1)
            dve.wait_ge(sm["cnt_done"], 1)
            V.tensor_scalar(cnt_i[:, :], cnt[:, :], float(P - 1), None, ALU.add).then_inc(sm["cnti_done"], 1)
            dve.wait_ge(sm["cnti_done"], 1)
            V.tensor_single_scalar(til_i[:, :], cnt_i[:, :], 7, op=ALU.arith_shift_right).then_inc(sm["tili_done"], 1)
            dve.wait_ge(sm["tili_done"], 1)
            V.tensor_copy(til[:, :], til_i[:, :]).then_inc(sm["til_done"], 1)
            dve.wait_ge(sm["til_done"], 1)
            V.tensor_tensor(cumm[:, :, :], til[:, :].unsqueeze(1).to_broadcast([1, E, E]),
                            const[0:1, C_CUM:C_CUM + E * E].rearrange("p (a b) -> p a b", a=E), ALU.mult
                            ).then_inc(sm["cumm_done"], 1)
            dve.wait_ge(sm["cumm_done"], 1)
            V.tensor_reduce(cum[:, :], cumm[:, :, :], AX.X, ALU.add).then_inc(sm["cum_done"], 1)
            dve.wait_ge(sm["cum_done"], 1)
            V.tensor_tensor(done[:, :, :], cum[:, :].unsqueeze(1).to_broadcast([1, MOE_TILES, E]),
                            const[0:1, C_TILE:C_TILE + MOE_TILES].unsqueeze(2).to_broadcast([1, MOE_TILES, E]),
                            ALU.is_le).then_inc(sm["dn_done"], 1)
            dve.wait_ge(sm["dn_done"], 1)
            V.tensor_tensor(donet[:, :, :], done[:, :, :], til[:, :].unsqueeze(1).to_broadcast([1, MOE_TILES, E]),
                            ALU.mult).then_inc(sm["dnt_done"], 1)
            V.tensor_reduce(eidx[:, :], done[:, :, :], AX.X, ALU.add).then_inc(sm["eidx_done"], 1)
            dve.wait_ge(sm["dnt_done"], 1)
            V.tensor_reduce(past[:, :], donet[:, :, :], AX.X, ALU.add).then_inc(sm["past_done"], 1)
            dve.wait_ge(sm["eidx_done"], 1)
            V.tensor_scalar(woff[:, :], eidx[:, :], float(E - 1), float(INTER), ALU.min, ALU.mult
                            ).then_inc(sm["plan_done"], 1)
            V.tensor_scalar(ereg[:, :], eidx[:, :], float(REGION), None, ALU.mult).then_inc(sm["ereg_done"], 1)
            dve.wait_ge(sm["past_done"], 1)
            V.tensor_tensor(row_f[:, :], const[0:1, C_TILE:C_TILE + MOE_TILES], past[:, :], ALU.subtract
                            ).then_inc(sm["row_done"], 1)
            dve.wait_ge(sm["row_done"], 1)
            dve.wait_ge(sm["ereg_done"], 1)
            V.scalar_tensor_tensor(ereg[:, :], row_f[:, :], float(P), ereg[:, :], ALU.mult, ALU.add
                                   ).then_inc(sm["ereg_done"], 1)
            dve.wait_ge(sm["ereg_done"], 2)
            V.tensor_scalar(rowoff[:, :], ereg[:, :], float(PAD_ROW), None, ALU.min).then_inc(sm["plan_done"], 1)

            def experts(s, p, live):
                q = 1 - p
                if live(0):
                    dve.wait_ge(xr_in[p], (s // 2) * 16 + 16 if isinstance(s, int) else (s - p) * 8 + 16)
                    if not isinstance(s, int) or s >= 2:
                        dve.wait_ge(sm["hid_done"], s - 1)
                    V.tensor_copy(wt_a[p][:, :], xrow[p][:, D:D + 1]).then_inc(sm["wta_done"], 1)
                    dve.wait_ge(sm["t32_done"], s + 1)
                    if not isinstance(s, int) or s >= 2:
                        dve.wait_ge(sm["u_ps"], s - 1)
                    V.tensor_copy(t_hi[p][:, :], t32[:, :]).then_inc(sm["thi_done"], 1)
                    dve.wait_ge(sm["thi_done"], s + 1)
                    V.tensor_tensor(t_lo[p][:, :], t32[:, :], t_hi[p][:, :].bitcast(F32), ALU.subtract
                                    ).then_inc(sm["tlo_done"], 1)
                if live(1):
                    i = s - 1
                    dve.wait_ge(sm["sg_done"], i + 1)
                    dve.wait_ge(sm["u_ps"], i + 1)
                    dve.wait_ge(sm["wta_done"], i + 1)
                    if not isinstance(s, int) or i >= 2:
                        dve.wait_ge(sm["hT_ps"], i - 1)
                    V.scalar_tensor_tensor(hid[q][:, :], sg[q][:, :], wt_a[q][:, :], banks[2 + q][:, :],
                                           ALU.mult, ALU.mult).then_inc(sm["hid_done"], 1)
                if live(2):
                    i = s - 2
                    dve.wait_ge(sm["hhi_done"], i + 1)
                    if not isinstance(s, int) or i >= 2:
                        dve.wait_ge(sm["y_ps"], i - 1)
                    V.tensor_tensor(h_lo[p][:, :], banks[4 + p][:, :], h_hi[p][:, :].bitcast(F32), ALU.subtract
                                    ).then_inc(sm["hlo_done"], 1)

            run_steps(dve, experts, MOE_TILES, 3)

            def finish(s, p, live):
                if live(0):
                    dve.wait_ge(y_in[p], (s // 2) * 16 + 16 if isinstance(s, int) else (s - p) * 8 + 16)
                    if not isinstance(s, int) or s >= 2:
                        dve.wait_ge(sm["o_done"], NT * (s - 1))
                    V.tensor_tensor(z[p][:, :, :], resid_v(s), yin[p][:, :, 0, :], ALU.add).then_inc(sm["z0_done"], 1)
                    dve.wait_ge(sm["z0_done"], s + 1)
                    V.tensor_tensor(z[p][:, :, :], z[p][:, :, :], yin[p][:, :, 1, :], ALU.add).then_inc(sm["z_done"], 1)
                    dve.wait_ge(sm["z_done"], s + 1)
                    for t in range(NT):
                        if not isinstance(s, int) or s >= 1:
                            dve.wait_ge(sm["mv3_done"], NT * s)
                        V.bn_stats(st3[:, t, :], z[p][:, t, :]).then_inc(sm["st3_done"], 1)
                    for t in range(NT):
                        dve.wait_ge(sm["st3_done"], NT * s + t + 1)
                        if not isinstance(s, int) or s >= 2:
                            dve.wait_ge(sm["vc_done"], s - 1)
                        V.bn_aggr(mv3[p][:, t, :], st3[:, t, :]).then_inc(sm["mv3_done"], 1)
                if live(1):
                    b, q = s - 1, 1 - p
                    dve.wait_ge(sm["rs3_done"], b + 1)
                    if not isinstance(s, int) or b >= 2:
                        dve.wait_ge(o_sent[q], (b // 2) * 16 if isinstance(b, int) else (b - q) * 8)
                    for t in range(NT):
                        V.tensor_scalar(osb[q][:, t, :], z[q][:, t, :], mv3[q][:, t, 0:1], rs3[q][:, t:t + 1],
                                        ALU.subtract, ALU.mult).then_inc(sm["o_done"], 1)

            straight_steps(finish, B, 1)

        @block.gpsimd
        def _(pool):
            G = nc.gpsimd
            G.memset(zero_i[:, :], 0).then_inc(sm["zero_ready"], 1)

            def split(s, p):
                pool.wait_ge(sm["w_hi"], s * 3 + 3)
                for j, (hi, lo) in enumerate(((wg_hi, wg_lo), (wu_hi, wu_lo), (wd_hi, wd_lo))):
                    cs = bass.ds(s * WP, WP)
                    last = G.tensor_tensor(lo[:, cs], w_raw[p][:, j, :], hi[:, cs].bitcast(F32), ALU.subtract)
                last.then_inc(sm["w_lo"], 1)

            def front(s, p, live):
                q = 1 - p
                if live(0):
                    pool.wait_ge(x_in[p], (s // 2) * 16 + 16 if isinstance(s, int) else (s - p) * 8 + 16)
                    if isinstance(s, int) and s == 0:
                        pool.wait_ge(sm["bias_ready"], 1)
                    G.tensor_tensor(resid(s), xin[p][:, :, :].rearrange("p t d -> p (t d)"),
                                    bias_out[:, :, :].rearrange("p t d -> p (t d)"), ALU.add
                                    ).then_inc(sm["xb_done"], 1)
                if live(2):
                    b = s - 2
                    pool.wait_ge(sm["mv0_done"], NT * b + NT)
                    if isinstance(s, int) and b == 0:
                        pool.wait_ge(sm["half_ready"], 1)
                    if not isinstance(s, int) or b >= 1:
                        pool.wait_ge(sm["rs0_done"], b)
                    G.tensor_scalar(va[:, 0, :], mv0[p][:, :, 1], EPS, None, ALU.add).then_inc(sm["va_done"], 1)
                    G.tensor_scalar(va[:, 1, :], mv0[p][:, :, 1], 1.0 + EPS, EPS * EPS, ALU.mult, ALU.add
                                    ).then_inc(sm["va_done"], 1)
                    pool.wait_ge(sm["va_done"], 2 * b + 2)
                    if not isinstance(s, int) or b >= 2:
                        pool.wait_ge(sm["x1_done"], NT * (b - 1))
                        pool.wait_ge(sm["n1_done"], NT * (b - 1))
                    G.tensor_tensor(rs0[p][:, :, :].rearrange("p a t -> p (a t)"),
                                    va[:, :, :].rearrange("p a t -> p (a t)"), mhalf[:, :], ALU.pow
                                    ).then_inc(sm["rs0_done"], 1)
                if live(3):
                    b = s - 3
                    pool.wait_ge(sm["mv2_done"], NT * b + NT)
                    if not isinstance(s, int) or b >= 1:
                        pool.wait_ge(sm["rs2_done"], b)
                    G.tensor_scalar(vb[:, :], mv2[q][:, :, 1], EPS, None, ALU.add).then_inc(sm["vb_done"], 1)
                    pool.wait_ge(sm["vb_done"], b + 1)
                    if not isinstance(s, int) or b >= 2:
                        pool.wait_ge(sm["n2_done"], NT * (b - 1))
                    G.tensor_tensor(rs2[q][:, :], vb[:, :], mhalf[:, 0:NT], ALU.pow).then_inc(sm["rs2_done"], 1)
                    pool.wait_ge(sm["h_done"], b + 1)
                    pool.wait_ge(sm["n1_done"], NT * b + NT)
                    G.tensor_tensor(resid(b), x1[q][:, :, :].rearrange("p t d -> p (t d)"),
                                    h[q][:, :, :].rearrange("p t d -> p (t d)"), ALU.add).then_inc(sm["res_done"], 1)
                if live(4):
                    b = s - 4
                    pool.wait_ge(sm["place_done"], b + 1)
                    pool.wait_ge(sm["meta_done"], 2 * b + 2)
                    pool.wait_ge(sm["n2_done"], NT * b + NT)
                    for t in range(NT):
                        for k in range(TOPK):
                            G.indirect_dma_start(
                                out=expert_rows[:, :],
                                out_offset=bass.IndirectOffsetOnAxis(ap=place[p][:, t, k:k + 1], axis=0),
                                in_=rows[p][:, t, k, :], in_offset=None).then_inc(sent[p], 16)
                if live(0):
                    split(s, p)

            straight_steps(front, B, LAST)

            def experts(s, p, live):
                q = 1 - p
                if live(3):
                    i = s - 3
                    n = pool.snap(i + 1)
                    if not isinstance(s, int) or i >= 2:
                        pool.wait_ge(y_sent[q], (i // 2) * 16 if isinstance(i, int) else (i - q) * 8)
                    pool.wait_ge(sm["idxa_done"], n)
                    G.tensor_tensor(idx_b[q][:, :], idx_a[q][:, :], zero_i[:, :], ALU.add
                                    ).then_inc(sm["idxb_done"], 1)
                    pool.wait_ge(sm["zero_ready"], 1)
                    pool.wait_ge(sm["idxb_done"], n)
                    pool.wait_ge(sm["ysb_done"], n)
                    G.indirect_dma_start(
                        out=moe_rows[:, :], out_offset=bass.IndirectOffsetOnAxis(ap=idx_b[q][:, :], axis=0),
                        in_=ysb[q][:, :], in_offset=None, bounds_check=Y_ROWS - 1, oob_is_err=False
                    ).then_inc(y_sent[q], 16)
                if live(1):
                    i = s - 1
                    pool.wait_ge(xr_in[q], (i // 2) * 16 + 16 if isinstance(i, int) else (i - q) * 8 + 16)
                    G.tensor_tensor(idx_a[q][:, :], xrow[q][:, D + 1:D + 2].bitcast(I32), zero_i[:, :], ALU.add
                                    ).then_inc(sm["idxa_done"], 1)

            run_steps(pool, experts, MOE_TILES, 3)

            def finish(s, p, live):
                if live(0):
                    pool.wait_ge(sm["mv3_done"], NT * s + NT)
                    if not isinstance(s, int) or s >= 1:
                        pool.wait_ge(sm["rs3_done"], s)
                    G.tensor_scalar(vc[:, :], mv3[p][:, :, 1], EPS, None, ALU.add).then_inc(sm["vc_done"], 1)
                    pool.wait_ge(sm["vc_done"], s + 1)
                    if not isinstance(s, int) or s >= 2:
                        pool.wait_ge(sm["o_done"], NT * (s - 1))
                    G.tensor_tensor(rs3[p][:, :], vc[:, :], mhalf[:, 0:NT], ALU.pow).then_inc(sm["rs3_done"], 1)

            straight_steps(finish, B, 1)


def kernel(**inputs):
    import concourse.bacc as bacc
    from concourse.bass_utils import run_bass_kernel_spmd

    a = {n[3:]: np.asarray(v) for n, v in inputs.items()}
    wqkv, bqkv = a["attn_W_qkv"], a["attn_b_qkv"]
    cols = [bqkv[0:D], bqkv[D:2 * D], bqkv[2 * D:], a["ffn_ln1_g"], a["ffn_ln1_b"], a["ffn_ln2_g"], a["ffn_ln2_b"]]
    par = np.concatenate([wqkv[:, 0:2 * D], wqkv[:, 2 * D:].T, a["attn_W_out"], a["ffn_attn_w"].T,
                          a["ffn_gate_w"].T, np.broadcast_to(a["attn_b_out"], (P, D)),
                          np.stack(cols, axis=1)], axis=1)
    arrays = {
        "x": np.ascontiguousarray(a["attn_x"]),
        "par": np.ascontiguousarray(par),
        "con": constants(),
        "dst": destinations(),
        "weights": np.ascontiguousarray(np.concatenate([
            a["ffn_gate_proj"].reshape(E * INTER, D).T, a["ffn_up_proj"].reshape(E * INTER, D).T,
            a["ffn_down_proj"].reshape(E, D, NC, P).transpose(3, 0, 2, 1).reshape(P, E * INTER)], axis=1)),
    }
    nc = bacc.Bacc("TRN2", target_bir_lowering=False, num_devices=1)
    aps = {n: nc.dram_tensor(n, v.shape, mybir.dt.from_np(v.dtype), kind="ExternalInput").ap()
           for n, v in arrays.items()}
    out = nc.dram_tensor("out", (B, S, D), F32, kind="ExternalOutput").ap()
    block_kernel(nc, out=out, **aps)
    r = run_bass_kernel_spmd(nc, [arrays], core_ids=[0])
    return r.results[0]["out"]
```

```python
import concourse.bass as bass
import concourse.mybir as mybir
from contextlib import ExitStack
import numpy as np

F32 = mybir.dt.float32
F32R = mybir.dt.float32r
BF16 = mybir.dt.bfloat16
I32 = mybir.dt.int32
U32 = mybir.dt.uint32
ALU = mybir.AluOpType
ACT = mybir.ActivationFunctionType
AX = mybir.AxisListType

B, S, D = 16, 256, 128
P = 128
NT = S // P
T = B * S
E, TOPK, INTER = 8, 2, 512
NC = INTER // P
EPS = 1e-5
QSCALE = float(D) ** -0.5
ROW = D + 2
REGION = T + P
PAD_ROW = E * REGION
X_ROWS = PAD_ROW + P
Y_ROWS = T * TOPK
MOE_TILES = T * TOPK // P + E - 1
TOKEN_TILES = T // P

WQ, WK, WVT, WO, AW, GW = 0, 128, 256, 384, 512, 640
BOUT = 648
BQ, BK, BV, G1, B1, G2, B2 = range(776, 783)
NPAR = 783
C_ID, C_TRI, C_ONE, C_IOTA8, C_BASE, C_TILE, C_CUM = 0, 128, 256, 384, 392, 400, 471
NCON = 471 + 64


def constants():
    c = np.zeros((P, NCON), np.float32)
    c[:, C_ID:C_ID + P] = np.eye(P)
    c[:, C_TRI:C_TRI + P] = np.triu(np.ones((P, P)), 1)
    c[:, C_ONE:C_ONE + P] = 1.0
    c[:, C_IOTA8:C_IOTA8 + E] = np.arange(E)
    c[:, C_BASE:C_BASE + E] = np.arange(E) * REGION
    c[:, C_TILE:C_TILE + MOE_TILES] = np.arange(MOE_TILES)
    c[:, C_CUM:C_CUM + E * E] = np.tril(np.ones((E, E))).reshape(-1)
    return c


def destinations():
    p = np.arange(P)[:, None, None]
    t = np.arange(TOKEN_TILES)[None, :, None]
    d = (p + P * t) * TOPK + np.arange(TOPK)[None, None, :]
    fill = Y_ROWS + np.arange(P)[:, None]
    return np.concatenate([d.reshape(P, -1), fill], axis=1).astype(np.int32)


NDST = TOKEN_TILES * TOPK + 1

RING = 4
UNROLL = 8
NX = 5
NWR = 4
NR = 4


def block_kernel(nc, x, par, con, dst, weights, out):
    x_v = x.rearrange("b (t p) d -> b p t d", p=P)
    w_v = weights.rearrange("p (j n) -> p j n", j=3)
    out_v = out.rearrange("b (t p) d -> b p t d", p=P)
    expert_rows = nc.dram_tensor("expert_rows", [X_ROWS, ROW], F32, kind="Internal").ap()
    moe_rows = nc.dram_tensor("moe_rows", [Y_ROWS, D], F32, kind="Internal").ap()
    moe_v = moe_rows.rearrange("(b t p k) d -> b p t (k d)", p=P, k=TOPK, t=NT)

    with ExitStack() as ctx:
        def sb(name, shape, dt=F32):
            return ctx.enter_context(nc.sbuf_tensor(name, shape, dt))

        def ring(name, shape, dt=F32, n=2):
            return [sb(f"{name}{i}", shape, dt) for i in range(n)]

        def sem(name):
            return ctx.enter_context(nc.semaphore(name))

        params = sb("params", [P, NPAR])
        const = sb("const", [P, NCON])
        dests = sb("dests", [P, NDST], I32)
        tri = sb("tri", [P, P], BF16)
        ones = sb("ones", [P, P], BF16)
        wvo = sb("wvo", [P, D])
        bq_s = sb("bq_s", [P, 1])
        bv_wide = sb("bv_wide", [P, P])
        bias_out = sb("bias_out", [P, NT, D])
        mhalf = sb("mhalf", [P, 2 * NT])
        xin = ring("xin", [P, NT, D], n=NX)
        xT = ring("xT", [P, S])
        qT = ring("qT", [P, S])
        kT = ring("kT", [P, S])
        vo = ring("vo", [P, NT, D], n=3)
        prob = ring("prob", [P, NT, S])
        probT = ring("probT", [P, NT, S])
        y = ring("y", [P, NT, D])
        n1 = ring("n1", [P, NT, D])
        n1T = ring("n1T", [P, S])
        x1_all = sb("x1_all", [P, B, NT, D])
        h_all = sb("h_all", [P, B, NT, D])
        rows = ring("rows", [P, NT, TOPK, ROW], n=NR)
        tT = ring("tT", [P, S])
        negmax = ring("negmax", [P, NT])
        rsum = ring("rsum", [P, NT], n=3)
        rinv = ring("rinv", [P, NT])
        st0 = sb("st0", [P, NT, 6])
        mv0 = ring("mv0", [P, NT, 2])
        var0 = ring("var0", [P, 2, NT])
        rs0 = ring("rs0", [P, 2, NT])
        shift0 = ring("shift0", [P, NT])
        st2 = sb("st2", [P, NT, 6])
        mv2 = ring("mv2", [P, NT, 2])
        var2 = ring("var2", [P, NT])
        rs2 = ring("rs2", [P, NT])
        lg = sb("lg", [P, NT, E])
        top = ring("top", [P, NT, 8])
        topi = sb("topi", [P, NT, 8], U32)
        topf = sb("topf", [P, NT, TOPK])
        onehot = sb("onehot", [P, NT, TOPK, E])
        member = ring("member", [P, NT, E], BF16)
        base = sb("base", [P, E])
        slots = sb("slots", [P, NT, E])
        picked = sb("picked", [P, NT, TOPK, E])
        place = ring("place", [P, NT, TOPK], I32, n=NR)
        gap = ring("gap", [P, NT])
        ex = ring("ex", [P, NT])
        exp1 = sb("exp1", [P, NT])
        wts = sb("wts", [P, NT, TOPK])
        cnt = sb("cnt", [1, E])
        cnt_i = sb("cnt_i", [1, E], I32)
        til_i = sb("til_i", [1, E], I32)
        til = sb("til", [1, E])
        cumm = sb("cumm", [1, E, E])
        cum = sb("cum", [1, E])
        done = sb("done", [1, MOE_TILES, E])
        donet = sb("donet", [1, MOE_TILES, E])
        eidx = sb("eidx", [1, MOE_TILES])
        past = sb("past", [1, MOE_TILES])
        row_f = sb("row_f", [1, MOE_TILES])
        ereg = sb("ereg", [1, MOE_TILES])
        woff = sb("woff", [1, MOE_TILES], I32)
        rowoff = sb("rowoff", [1, MOE_TILES], I32)
        fill_at = sb("fill_at", [1, E], I32)
        fill = sb("fill", [P, ROW])
        NW = E * INTER
        WP = NW // B
        w_raw = ring("w_raw", [P, 2, WP], n=NWR)
        w_hi = sb("w_hi", [P, 2, NW], F32R)
        w_lo = sb("w_lo", [P, 2, NW], F32R)
        wd = sb("wd", [P, NW])
        xrow = ring("xrow", [P, ROW], n=RING)
        t32 = ring("t32", [P, P])
        t_hi = ring("t_hi", [P, P], F32R)
        t_lo = ring("t_lo", [P, P], F32R)
        sg = ring("sg", [P, INTER])
        hid = ring("hid", [P, INTER])
        hidT = ring("hidT", [P, INTER])
        warm = sb("warm", [P, 1])
        zero_i = sb("zero_i", [P, 1], I32)
        idx = ring("idx", [P, 1], I32, n=RING)
        ysb = ring("ysb", [P, D], n=RING)
        yin = ring("yin", [P, NT, TOPK, D], n=RING)
        st3 = sb("st3", [P, NT, 6])
        mv3 = ring("mv3", [P, NT, 2])
        var3 = ring("var3", [P, NT])
        rs3 = ring("rs3", [P, NT])
        shift3 = ring("shift3", [P, NT])

        banks = [ctx.enter_context(nc.psum_tensor(f"bank{i}", [P, 512], F32)) for i in range(8)]
        ps_q, ps_k = banks[0][:, 0:256], banks[0][:, 256:512]
        ps_v = banks[1][:, 0:256]
        ps_s = banks[2][:, :]
        ps_p = banks[3][:, :]
        ps_o = banks[4][:, 0:256]
        ps_a = banks[5][:, 0:256]
        ps_n2 = ps_n1 = ps_x = banks[6][:, 0:256]
        ps_l = banks[7][:, 0:NT * E].rearrange("p (t e) -> p t e", t=NT)
        ps_r = banks[7][:, 64:64 + NT * E].rearrange("p (t e) -> p t e", t=NT)
        ps_t = banks[7][:, 128:128 + E]
        ident = const[:, C_ID:C_ID + P]

        names = ("par_in con_in dst_in wd_in cast_done wvo_done wvo_copied bias_ready bq_ready bv_ready half_ready "
                 "xT_ps xT_sb k_ps q_sb v_ps v_sb s_ps max_done prob_done pT_ps pT_sb "
                 "o_ps rinv_done y_done st0_done mv0_done var0_done rs0_done shift0_done n1_done x1_done n1T_ps n1T_sb "
                 "a_ps h_done st2_done mv2_done var2_done rs2_done n2_done n2T_ps tT_sb l_ps lg_done "
                 "top_done topi_done topf_done onehot_done member_done gap_done ex_done exp1_done wts_done meta_done "
                 "t_ps slots_done picked_done place_done base_done base_init res_done "
                 "cnt_done cnti_done tili_done til_done cumm_done cum_done dn_done dnt_done eidx_done past_done "
                 "ereg_done row_done plan_done warm_done fill_ready fill_done odd_filled whi_done wlo_done "
                 "xr_ps t32_done thi_done tlo_done g_ps u_ps sg_done hid_done hT_ps hT_sb y_ps ysb_done "
                 "zero_ready idx_done "
                 "z0_done z_done st3_done mv3_done var3_done rs3_done shift3_done o_done").split()
        sm = {n: sem(n) for n in names}

        def sems(name, n=2):
            return [sem(f"{name}{i}") for i in range(n)]

        x_in, w_in, sent = sems("x_in", NX), sems("w_in", NWR), sems("sent", NR)
        xr_in, y_sent, y_in, o_sent = sems("xr_in", RING), sems("y_sent", RING), sems("y_in", RING), sems("o_sent", RING)

        block = ctx.enter_context(nc.Block())

        def straight_steps(step, n_items, depth):
            for s in range(n_items + depth):
                step(s, lambda lag, s=s: 0 <= s - lag < n_items)

        def looped_steps(eng, step, n_items, depth):
            first = -(-(depth + RING) // RING) * RING
            turns = (n_items - first) // UNROLL
            for s in range(first):
                step(s, s % RING, lambda lag, s=s: 0 <= s - lag < n_items)
            with eng.Fori(0, turns) as i:
                for r in range(UNROLL):
                    step(i * UNROLL + (first + r), r % RING, lambda lag: True)
            for s in range(first + UNROLL * turns, n_items + depth):
                step(s, s % RING, lambda lag, s=s: 0 <= s - lag < n_items)

        def far(i, n):
            return not isinstance(i, int) or i >= n

        def turn(i, place_, n=RING, per=16):
            return per * (i // n + 1) if isinstance(i, int) else (i - place_) * (per // n) + per

        PIECES = [3, 3, 2, 3, 0, 0, 0, 0, 0, 0, 0, 0, 0, 0, 1, 0, 1, 1, 1, 1, 0, 0]

        def pieces(s):
            if s >= len(PIECES):
                return ()
            return range(sum(PIECES[:s]), sum(PIECES[:s + 1]))

        FRONT = 6
        SCAT = 16 * NT * TOPK

        @block.sync
        def _(sp):
            def load_x(b):
                if b >= NX:
                    sp.wait_ge(sm["y_done"], NT * (b - NX) + NT)
                    sp.wait_ge(sm["xT_ps"], b - NX + 1)
                sp.dma_start(xin[b % NX][:, :, :], x_v[b]).then_inc(x_in[b % NX], 16)

            load_x(0)
            sp.dma_start(params[:, :], par).then_inc(sm["par_in"], 16)
            sp.dma_start(const[:, :], con).then_inc(sm["con_in"], 16)
            load_x(1)
            sp.dma_start(dests[:, :], dst).then_inc(sm["dst_in"], 16)

            def front(s, live):
                if 2 <= s < B:
                    load_x(s)
                for i in pieces(s):
                    if i >= NWR:
                        sp.wait_ge(sm["wlo_done"], i - NWR + 1)
                    sp.dma_start(w_raw[i % NWR][:, :, :], w_v[:, 0:2, i * WP:(i + 1) * WP]).then_inc(w_in[i % NWR], 16)

            straight_steps(front, B, FRONT)
            sp.dma_start(wd[:, :], w_v[:, 2, :]).then_inc(sm["wd_in"], 16)

            sp.wait_ge(sm["fill_ready"], 3)
            sp.dma_start(expert_rows[PAD_ROW:PAD_ROW + P, :], fill[:, :]).then_inc(sm["fill_done"], 16)
            sp.wait_ge(sm["plan_done"], 1)
            for e in range(0, E, 2):
                end = sp.value_load(fill_at[0:1, e:e + 1], min_val=0, max_val=X_ROWS - P)
                sp.dma_start(expert_rows[bass.ds(end, P), :], fill[:, :]).then_inc(sm["fill_done"], 16)
            sp.wait_ge(sm["plan_done"], 3)
            sp.wait_ge(sm["fill_done"], 16 * (E // 2 + 1))
            sp.wait_ge(sm["odd_filled"], 16 * (E // 2))
            for i in range(NR):
                sp.wait_ge(sent[i], SCAT * (B // NR))

            def load_rows(s, r, live):
                if live(0):
                    if far(s, RING):
                        sp.wait_ge(sm["hid_done"], s - (RING - 1))
                        sp.wait_ge(sm["idx_done"], s - (RING - 1))
                    at = sp.value_load(rowoff[0:1, bass.ds(s, 1)], min_val=0, max_val=X_ROWS - P)
                    sp.dma_start(xrow[r][:, :], expert_rows[bass.ds(at, P), :]).then_inc(xr_in[r], 16)

            looped_steps(sp, load_rows, MOE_TILES, 0)

            for r in range(RING):
                sp.wait_ge(y_sent[r], 16 * len(range(r, MOE_TILES, RING)))
            for b in range(B):
                if b >= RING:
                    sp.wait_ge(sm["z_done"], b - RING + 1)
                sp.dma_start(yin[b % RING][:, :, :, :].rearrange("p t k d -> p t (k d)"), moe_v[b]
                             ).then_inc(y_in[b % RING], 16)

        @block.tensor
        def _(pe):
            mm = nc.tensor.matmul
            pe.wait_ge(sm["par_in"], 16)
            pe.wait_ge(sm["con_in"], 16)
            mm(ps_o[:, 0:D], params[:, WVT:WVT + D], params[:, WO:WO + D], start=True, stop=True
               ).then_inc(sm["wvo_done"], 1)
            pe.wait_ge(sm["bv_ready"], 1)
            mm(ps_a[:, 0:D], bv_wide[:, :], params[:, WO:WO + D], start=True, stop=True
               ).then_inc(sm["wvo_done"], 1)

            def tok(t):
                return slice(t * P, (t + 1) * P)

            def front(s, live):
                if live(1):
                    b = s - 1
                    pe.wait_ge(sm["xT_sb"], b + 1)
                    if b >= 1:
                        pe.wait_ge(sm["q_sb"], 2 * b)
                        pe.wait_ge(sm["v_sb"], b)
                    xt = xT[b % 2]
                    mm(ps_q, params[:, WQ:WQ + D], xt[:, :], start=True, stop=True)
                    mm(ps_k, params[:, WK:WK + D], xt[:, :], start=True, stop=True).then_inc(sm["k_ps"], 1)
                    if b == 0:
                        pe.wait_ge(sm["wvo_copied"], 1)
                    for t in range(NT):
                        last = mm(ps_v[:, tok(t)], xt[:, tok(t)], wvo[:, :], start=True, stop=True)
                    last.then_inc(sm["v_ps"], 1)
                if live(2):
                    b = s - 2
                    pe.wait_ge(sm["prob_done"], NT * b + NT)
                    if b >= 1:
                        pe.wait_ge(sm["pT_sb"], b)
                    for kt in range(NT):
                        for t in range(NT):
                            last = nc.tensor.transpose(ps_p[:, kt * S + t * P:kt * S + (t + 1) * P],
                                                       prob[b % 2][:, t, kt * P:(kt + 1) * P], ident)
                    last.then_inc(sm["pT_ps"], 1)
                if live(0):
                    pe.wait_ge(x_in[s % NX], turn(s, s % NX, NX))
                    if s >= 6:
                        pe.wait_ge(sm["tT_sb"], s - 5)
                    elif s >= 5:
                        pe.wait_ge(sm["n1T_sb"], s - 4)
                    elif s >= 1:
                        pe.wait_ge(sm["xT_sb"], s)
                    for t in range(NT):
                        last = nc.tensor.transpose(ps_x[:, tok(t)], xin[s % NX][:, t, :], ident)
                    last.then_inc(sm["xT_ps"], 1)
                if live(3):
                    b = s - 3
                    pe.wait_ge(sm["pT_sb"], b + 1)
                    pe.wait_ge(sm["v_sb"], b + 1)
                    if b >= 1:
                        pe.wait_ge(sm["y_done"], NT * b)
                    for t in range(NT):
                        for kt in range(NT):
                            last = mm(ps_o[:, tok(t)], probT[b % 2][:, kt, tok(t)],
                                      vo[b % 3][:, kt, :], start=(kt == 0), stop=(kt == NT - 1))
                    last.then_inc(sm["o_ps"], 1)
                if live(6):
                    b = s - 6
                    m = member[b % 2]
                    if b == 0:
                        pe.wait_ge(sm["cast_done"], 2)
                    pe.wait_ge(sm["member_done"], b + 1)
                    for t in range(NT):
                        for u in range(t):
                            mm(ps_r[:, t, :], ones[:, :], m[:, u, :], start=(u == 0), stop=False)
                        mm(ps_r[:, t, :], tri[:, :], m[:, t, :], start=(t == 0), stop=True)
                    for t in range(NT):
                        last = mm(ps_t, ones[:, :], m[:, t, :], start=(t == 0), stop=(t == NT - 1))
                    last.then_inc(sm["t_ps"], 1)
                if live(4):
                    b = s - 4
                    pe.wait_ge(sm["n1_done"], NT * b + NT)
                    pe.wait_ge(sm["xT_sb"], min(s + 1, B))
                    for t in range(NT):
                        last = nc.tensor.transpose(ps_n1[:, tok(t)], n1[b % 2][:, t, :], ident)
                    last.then_inc(sm["n1T_ps"], 1)
                if live(1):
                    b = s - 1
                    pe.wait_ge(sm["q_sb"], 2 * b + 2)
                    if b >= 1:
                        pe.wait_ge(sm["prob_done"], NT * b)
                    for t in range(NT):
                        last = mm(ps_s[:, t * S:(t + 1) * S], qT[b % 2][:, tok(t)], kT[b % 2][:, :],
                                  start=True, stop=True)
                    last.then_inc(sm["s_ps"], 1)
                if live(5):
                    b = s - 5
                    pe.wait_ge(sm["n2_done"], NT * b + NT)
                    pe.wait_ge(sm["n1T_sb"], min(b + 2, B))
                    for t in range(NT):
                        last = nc.tensor.transpose(ps_n2[:, tok(t)], rows[b % NR][:, t, 0, 0:D], ident)
                    last.then_inc(sm["n2T_ps"], 1)
                if live(4):
                    b = s - 4
                    pe.wait_ge(sm["n1T_sb"], b + 1)
                    pe.wait_ge(sm["h_done"], b) if b >= 1 else pe.wait_ge(sm["bias_ready"], 1)
                    for t in range(NT):
                        last = mm(ps_a[:, tok(t)], n1T[b % 2][:, tok(t)], params[:, AW:AW + D],
                                  start=True, stop=True)
                    last.then_inc(sm["a_ps"], 1)
                if live(5):
                    b = s - 5
                    pe.wait_ge(sm["tT_sb"], b + 1)
                    if b >= 1:
                        pe.wait_ge(sm["base_done"], b)
                    for t in range(NT):
                        last = mm(ps_l[:, t, :], tT[b % 2][:, tok(t)], params[:, GW:GW + E], start=True, stop=True)
                    last.then_inc(sm["l_ps"], 1)

            straight_steps(front, B, FRONT)

            pe.wait_ge(sm["wlo_done"], B)
            pe.wait_ge(sm["wd_in"], 16)
            pe.wait_ge(sm["base_done"], B)
            pe.wait_ge(sm["h_done"], B)
            pe.wait_ge(sm["tT_sb"], B)
            pe.wait_ge(sm["plan_done"], 3)

            gate_reg = pe.alloc_register("gate_at")

            def gate_up(w, j, bank, i2):
                mm(bank[:, :], t_hi[i2][:, :], w_hi[:, j, w], start=True, stop=False)
                mm(bank[:, :], t_hi[i2][:, :], w_lo[:, j, w], start=False, stop=False)
                return mm(bank[:, :], t_lo[i2][:, :], w_hi[:, j, w], start=False, stop=True)

            def experts(s, r, live):
                if live(1):
                    w_gate = pe.snap(gate_reg).with_bounds(min_val=0, max_val=(E - 1) * INTER)
                if live(0):
                    pe.wait_ge(xr_in[r], turn(s, r))
                    if far(s, 1):
                        pe.wait_ge(sm["t32_done"], s)
                    nc.tensor.transpose(banks[6][:, 0:P], xrow[r][:, 0:D], ident).then_inc(sm["xr_ps"], 1)
                if live(1):
                    i, i2 = s - 1, (r - 1) % 2
                    w = w_gate
                    pe.wait_ge(sm["tlo_done"], i + 1)
                    if far(i, 2):
                        pe.wait_ge(sm["hid_done"], i - 1)
                    gate_up(bass.ds(w, INTER), 0, banks[i2], i2).then_inc(sm["g_ps"], 1)
                    gate_up(bass.ds(w, INTER), 1, banks[2 + i2], i2).then_inc(sm["u_ps"], 1)
                if live(0):
                    pe.reg_load(gate_reg, woff[0:1, bass.ds(s, 1)])
                if live(2):
                    i, i2 = s - 2, r % 2
                    pe.wait_ge(sm["hid_done"], i + 1)
                    if far(i, 2):
                        pe.wait_ge(sm["hT_sb"], i - 1)
                    for c in range(NC):
                        last = nc.tensor.transpose(banks[4 + i2][:, c * P:(c + 1) * P],
                                                   hid[i2][:, c * P:(c + 1) * P], ident)
                    last.then_inc(sm["hT_ps"], 1)
                if live(3):
                    i, i2 = s - 3, (r - 3) % 2
                    w = pe.value_load(woff[0:1, bass.ds(i, 1)], min_val=0, max_val=(E - 1) * INTER)
                    pe.wait_ge(sm["hT_sb"], i + 1)
                    if far(i, 1):
                        pe.wait_ge(sm["ysb_done"], i)
                    for c in range(NC):
                        last = mm(banks[7][:, 0:P], hidT[i2][:, c * P:(c + 1) * P],
                                  wd[:, bass.ds(w + c * P, P)], start=(c == 0), stop=(c == NC - 1))
                    last.then_inc(sm["y_ps"], 1)

            looped_steps(pe, experts, MOE_TILES, 3)

        @block.scalar
        def _(act):
            A = nc.scalar.activation
            col = lambda c: params[:, c:c + 1]
            flat = lambda a: a[:, :, :].rearrange("p t d -> p (t d)")
            act.wait_ge(sm["par_in"], 16)
            nc.scalar.mul(bq_s[:, :], col(BQ), QSCALE).then_inc(sm["bq_ready"], 1)
            act.wait_ge(sm["wvo_done"], 1)
            A(wvo[:, :], ps_o[:, 0:D], ACT.Copy).then_inc(sm["wvo_copied"], 1)
            act.wait_ge(sm["bq_ready"], 1)

            def front(s, live):
                if live(1):
                    b = s - 1
                    act.wait_ge(sm["k_ps"], b + 1)
                    if b >= 2:
                        act.wait_ge(sm["s_ps"], b - 1)
                    A(qT[b % 2][:, :], ps_q, ACT.Identity, bias=bq_s[:, :], scale=QSCALE).then_inc(sm["q_sb"], 1)
                    A(kT[b % 2][:, :], ps_k, ACT.Identity, bias=col(BK)).then_inc(sm["q_sb"], 1)
                if live(2):
                    b = s - 2
                    act.wait_ge(sm["pT_ps"], b + 1)
                    if b >= 2:
                        act.wait_ge(sm["o_ps"], b - 1)
                    A(flat(probT[b % 2]), ps_p, ACT.Copy).then_inc(sm["pT_sb"], 1)
                if live(6):
                    b = s - 6
                    act.wait_ge(sm["gap_done"], b + 1)
                    if b >= 2:
                        act.wait_ge(sm["wts_done"], 2 * (b - 1))
                    A(ex[b % 2][:, :], gap[b % 2][:, :], ACT.Exp).then_inc(sm["ex_done"], 1)
                if live(0):
                    act.wait_ge(sm["xT_ps"], s + 1)
                    if s >= 2:
                        act.wait_ge(sm["v_ps"], s - 1)
                    A(xT[s % 2][:, :], ps_x, ACT.Copy).then_inc(sm["xT_sb"], 1)
                if live(4):
                    b = s - 4
                    act.wait_ge(sm["shift0_done"], b + 1)
                    act.wait_ge(sm["y_done"], NT * b + NT)
                    act.wait_ge(sm["rs0_done"], b + 1)
                    for t in range(NT):
                        A(x1_all[:, b, t, :], y[b % 2][:, t, :], ACT.Identity, bias=shift0[b % 2][:, t:t + 1],
                          scale=rs0[b % 2][:, 0, t:t + 1]).then_inc(sm["x1_done"], 1)
                if live(4):
                    b = s - 4
                    act.wait_ge(sm["n1T_ps"], b + 1)
                    if b >= 2:
                        act.wait_ge(sm["a_ps"], b - 1)
                    A(n1T[b % 2][:, :], ps_n1, ACT.Identity, bias=col(B1), scale=col(G1)).then_inc(sm["n1T_sb"], 1)
                if live(5):
                    b = s - 5
                    act.wait_ge(sm["n2T_ps"], b + 1)
                    if b >= 2:
                        act.wait_ge(sm["l_ps"], b - 1)
                    A(tT[b % 2][:, :], ps_n2, ACT.Identity, bias=col(B2), scale=col(G2)).then_inc(sm["tT_sb"], 1)
                for i in pieces(s):
                    act.wait_ge(w_in[i % NWR], turn(i, i % NWR, NWR))
                    A(w_hi[:, :, i * WP:(i + 1) * WP], w_raw[i % NWR][:, :, :], ACT.Copy).then_inc(sm["whi_done"], 1)
                if live(1):
                    b = s - 1
                    act.wait_ge(sm["max_done"], b + 1)
                    if b >= 2:
                        act.wait_ge(sm["pT_ps"], b - 1)
                    if b >= 3:
                        act.wait_ge(sm["rinv_done"], b - 2)
                    for t in range(NT):
                        A(prob[b % 2][:, t, :], ps_s[:, t * S:(t + 1) * S], ACT.Exp,
                          bias=negmax[b % 2][:, t:t + 1], accum_out=rsum[b % 3][:, t:t + 1]
                          ).then_inc(sm["prob_done"], 1)

            straight_steps(front, B, FRONT)

            act.wait_ge(sm["plan_done"], 1)
            A(warm[:, :], bq_s[:, :], ACT.Silu).then_inc(sm["warm_done"], 1)
            for e in range(1, E, 2):
                end = act.value_load(fill_at[0:1, e:e + 1], min_val=0, max_val=X_ROWS - P)
                act.dma_start(expert_rows[bass.ds(end, P), :], fill[:, :]).then_inc(sm["odd_filled"], 16)

            def experts(s, r, live):
                if live(0):
                    act.wait_ge(sm["xr_ps"], s + 1)
                    if far(s, 2):
                        act.wait_ge(sm["tlo_done"], s - 1)
                    A(t32[r % 2][:, :], banks[6][:, 0:P], ACT.Identity, bias=col(B2),
                      scale=col(G2)).then_inc(sm["t32_done"], 1)
                if live(1):
                    i, i2 = s - 1, (r - 1) % 2
                    act.wait_ge(sm["g_ps"], i + 1)
                    if far(i, 2):
                        act.wait_ge(sm["hid_done"], i - 1)
                    A(sg[i2][:, :], banks[i2][:, :], ACT.Silu).then_inc(sm["sg_done"], 1)
                if live(3):
                    i, r3 = s - 3, (r - 3) % RING
                    act.wait_ge(sm["y_ps"], i + 1)
                    if far(i, RING):
                        act.wait_ge(y_sent[r3], turn(i, r3) - 16)
                    A(ysb[r3][:, :], banks[7][:, 0:P], ACT.Copy).then_inc(sm["ysb_done"], 1)

            looped_steps(act, experts, MOE_TILES, 3)

            def finish(s, live):
                if live(1):
                    b = s - 1
                    act.wait_ge(sm["shift3_done"], b + 1)
                    act.wait_ge(sm["rs3_done"], b + 1)
                    for t in range(NT):
                        A(x1_all[:, b, t, :], x1_all[:, b, t, :], ACT.Identity,
                          bias=shift3[b % 2][:, t:t + 1], scale=rs3[b % 2][:, t:t + 1]).then_inc(sm["o_done"], 1)
                    act.wait_ge(sm["o_done"], NT * b + NT)
                    act.dma_start(out_v[b], x1_all[:, b, :, :]).then_inc(o_sent[b % RING], 16)

            straight_steps(finish, B, 1)
            for i in range(RING):
                act.wait_ge(o_sent[i], 16 * (B // RING))

        @block.vector
        def _(dve):
            V = nc.vector
            flat = lambda a: a[:, :, :].rearrange("p t d -> p (t d)")
            dve.wait_ge(sm["par_in"], 16)
            V.tensor_copy(bv_wide[:, :], params[:, BV:BV + 1].to_broadcast([P, P])).then_inc(sm["bv_ready"], 1)
            V.memset(mhalf[:, :], -0.5).then_inc(sm["half_ready"], 1)
            dve.wait_ge(sm["con_in"], 16)
            V.tensor_copy(tri[:, :], const[:, C_TRI:C_TRI + P]).then_inc(sm["cast_done"], 1)
            V.tensor_copy(ones[:, :], const[:, C_ONE:C_ONE + P]).then_inc(sm["cast_done"], 1)
            V.tensor_copy(base[:, :], const[:, C_BASE:C_BASE + E]).then_inc(sm["base_init"], 1)
            dve.wait_ge(sm["wvo_done"], 2)
            V.tensor_tensor(bias_out[:, :, :], ps_a[:, 0:D].unsqueeze(1).to_broadcast([P, NT, D]),
                            params[:, BOUT:BOUT + D].unsqueeze(1).to_broadcast([P, NT, D]),
                            ALU.add).then_inc(sm["bias_ready"], 1)
            dve.wait_ge(sm["bias_ready"], 1)
            dve.wait_ge(sm["dst_in"], 16)
            V.memset(fill[:, 0:ROW], 0.0).then_inc(sm["fill_ready"], 1)
            dve.wait_ge(sm["fill_ready"], 1)
            V.tensor_copy(fill[:, D + 1:D + 2].bitcast(I32), dests[:, NDST - 1:NDST]).then_inc(sm["fill_ready"], 2)

            def front(s, live):
                if live(4):
                    b = s - 4
                    dve.wait_ge(sm["rs0_done"], b + 1)
                    V.scalar_tensor_tensor(shift0[b % 2][:, :], mv0[b % 2][:, :, 0], -1.0, rs0[b % 2][:, 0, :],
                                           ALU.mult, ALU.mult).then_inc(sm["shift0_done"], 1)
                    if b >= 2:
                        dve.wait_ge(sm["n1T_ps"], b - 1)
                    for t in range(NT):
                        V.tensor_scalar(n1[b % 2][:, t, :], y[b % 2][:, t, :], mv0[b % 2][:, t, 0:1],
                                        rs0[b % 2][:, 1, t:t + 1], ALU.subtract, ALU.mult).then_inc(sm["n1_done"], 1)
                if live(1):
                    b = s - 1
                    dve.wait_ge(sm["v_ps"], b + 1)
                    if b >= 3:
                        dve.wait_ge(sm["o_ps"], b - 2)
                    V.tensor_tensor(flat(vo[b % 3]), ps_v, flat(bias_out), ALU.add).then_inc(sm["v_sb"], 1)
                if live(5):
                    b = s - 5
                    dve.wait_ge(sm["rs2_done"], b + 1)
                    if b >= NR:
                        dve.wait_ge(sent[b % NR], turn(b, b % NR, NR, SCAT) - SCAT)
                        dve.wait_ge(sm["n2T_ps"], b - NR + 1)
                    for t in range(NT):
                        V.tensor_scalar(rows[b % NR][:, t, :, 0:D],
                                        h_all[:, b, t, :].unsqueeze(1).to_broadcast([P, TOPK, D]),
                                        mv2[b % 2][:, t, 0:1], rs2[b % 2][:, t:t + 1],
                                        ALU.subtract, ALU.mult).then_inc(sm["n2_done"], 1)
                if live(6):
                    b = s - 6
                    dve.wait_ge(sm["t_ps"], b + 1)
                    dve.wait_ge(sm["base_done"], b) if b >= 1 else dve.wait_ge(sm["base_init"], 1)
                    V.tensor_tensor(slots[:, :, :], ps_r, base[:, :].unsqueeze(1).to_broadcast([P, NT, E]),
                                    ALU.add).then_inc(sm["slots_done"], 1)
                    dve.wait_ge(sm["ex_done"], b + 1)
                    V.tensor_scalar(exp1[:, :], ex[b % 2][:, :], 1.0, None, ALU.add).then_inc(sm["exp1_done"], 1)
                    dve.wait_ge(sm["slots_done"], b + 1)
                    V.tensor_tensor(picked[:, :, :, :], onehot[:, :, :, :],
                                    slots[:, :, :].unsqueeze(2).to_broadcast([P, NT, TOPK, E]), ALU.mult
                                    ).then_inc(sm["picked_done"], 1)
                    V.tensor_tensor(base[:, :], ps_t, base[:, :], ALU.add).then_inc(sm["base_done"], 1)
                    dve.wait_ge(sm["exp1_done"], b + 1)
                    V.reciprocal(wts[:, :, 0], exp1[:, :]).then_inc(sm["wts_done"], 1)
                    if b >= NR:
                        dve.wait_ge(sent[b % NR], turn(b, b % NR, NR, SCAT) - SCAT)
                    dve.wait_ge(sm["picked_done"], b + 1)
                    with nc.allow_low_precision(reason="whole numbers below 2**24"):
                        V.tensor_reduce(place[b % NR][:, :, :], picked[:, :, :, :], AX.X, ALU.add
                                        ).then_inc(sm["place_done"], 1)
                    dve.wait_ge(sm["wts_done"], 2 * b + 1)
                    V.tensor_tensor(wts[:, :, 1], wts[:, :, 0], ex[b % 2][:, :], ALU.mult).then_inc(sm["wts_done"], 1)
                    V.tensor_copy(rows[b % NR][:, :, :, D + 1].bitcast(I32),
                                  dests[:, b * NT * TOPK:(b + 1) * NT * TOPK].rearrange("p (t k) -> p t k", t=NT)
                                  ).then_inc(sm["meta_done"], 1)
                    dve.wait_ge(sm["wts_done"], 2 * b + 2)
                    V.tensor_copy(rows[b % NR][:, :, :, D], wts[:, :, :]).then_inc(sm["meta_done"], 1)
                if live(3):
                    b = s - 3
                    dve.wait_ge(sm["prob_done"], NT * b + NT)
                    V.reciprocal(rinv[b % 2][:, :], rsum[b % 3][:, :]).then_inc(sm["rinv_done"], 1)
                    dve.wait_ge(sm["rinv_done"], b + 1)
                    dve.wait_ge(x_in[b % NX], turn(b, b % NX, NX))
                    dve.wait_ge(sm["o_ps"], b + 1)
                    if b >= 2:
                        dve.wait_ge(sm["x1_done"], NT * (b - 1))
                    for t in range(NT):
                        V.scalar_tensor_tensor(y[b % 2][:, t, :], ps_o[:, t * P:(t + 1) * P], rinv[b % 2][:, t:t + 1],
                                               xin[b % NX][:, t, :], ALU.mult, ALU.add).then_inc(sm["y_done"], 1)
                if live(3):
                    b = s - 3
                    for t in range(NT):
                        dve.wait_ge(sm["y_done"], NT * b + t + 1)
                        V.bn_stats(st0[:, t, :], y[b % 2][:, t, :]).then_inc(sm["st0_done"], 1)
                if live(1):
                    b = s - 1
                    dve.wait_ge(sm["s_ps"], b + 1)
                    if b >= 2:
                        dve.wait_ge(sm["prob_done"], NT * (b - 1))
                    V.tensor_reduce(negmax[b % 2][:, :], ps_s.rearrange("p (t k) -> p t k", t=NT), AX.X, ALU.max,
                                    negate=True).then_inc(sm["max_done"], 1)
                if live(3):
                    b = s - 3
                    for t in range(NT):
                        dve.wait_ge(sm["st0_done"], NT * b + t + 1)
                        V.bn_aggr(mv0[b % 2][:, t, :], st0[:, t, :]).then_inc(sm["mv0_done"], 1)
                if live(4):
                    b = s - 4
                    dve.wait_ge(sm["a_ps"], b + 1)
                    dve.wait_ge(sm["x1_done"], NT * b + NT)
                    V.tensor_tensor(h_all[:, b, :, :].rearrange("p t d -> p (t d)"), ps_a,
                                    x1_all[:, b, :, :].rearrange("p t d -> p (t d)"), ALU.add).then_inc(sm["h_done"], 1)
                if live(3):
                    b = s - 3
                    dve.wait_ge(sm["mv0_done"], NT * b + NT)
                    if b >= 2:
                        dve.wait_ge(sm["rs0_done"], b - 1)
                    V.tensor_scalar(var0[b % 2][:, 0, :], mv0[b % 2][:, :, 1], EPS, None, ALU.add
                                    ).then_inc(sm["var0_done"], 1)
                    V.tensor_scalar(var0[b % 2][:, 1, :], mv0[b % 2][:, :, 1], 1.0 + EPS, EPS * EPS, ALU.mult, ALU.add
                                    ).then_inc(sm["var0_done"], 1)
                if live(4):
                    b = s - 4
                    dve.wait_ge(sm["h_done"], b + 1)
                    for t in range(NT):
                        V.bn_stats(st2[:, t, :], h_all[:, b, t, :]).then_inc(sm["st2_done"], 1)
                if live(4):
                    b = s - 4
                    for t in range(NT):
                        dve.wait_ge(sm["st2_done"], NT * b + t + 1)
                        V.bn_aggr(mv2[b % 2][:, t, :], st2[:, t, :]).then_inc(sm["mv2_done"], 1)
                if live(4):
                    b = s - 4
                    dve.wait_ge(sm["mv2_done"], NT * b + NT)
                    if b >= 2:
                        dve.wait_ge(sm["rs2_done"], b - 1)
                    V.tensor_scalar(var2[b % 2][:, :], mv2[b % 2][:, :, 1], EPS, None, ALU.add).then_inc(sm["var2_done"], 1)
                for i in pieces(s):
                    dve.wait_ge(sm["whi_done"], i + 1)
                    cs = slice(i * WP, (i + 1) * WP)
                    V.tensor_tensor(w_lo[:, :, cs], w_raw[i % NWR][:, :, :], w_hi[:, :, cs].bitcast(F32),
                                    ALU.subtract).then_inc(sm["wlo_done"], 1)
                if live(5):
                    b = s - 5
                    dve.wait_ge(sm["l_ps"], b + 1)
                    V.tensor_copy(lg[:, :, :], ps_l).then_inc(sm["lg_done"], 1)
                    dve.wait_ge(sm["lg_done"], b + 1)
                    for t in range(NT):
                        V.max(top[b % 2][:, t, :], lg[:, t, :]).then_inc(sm["top_done"], 1)
                    for t in range(NT):
                        dve.wait_ge(sm["top_done"], NT * b + t + 1)
                        V.max_index(topi[:, t, :], top[b % 2][:, t, :], lg[:, t, :]).then_inc(sm["topi_done"], 1)
                    if b >= 2:
                        dve.wait_ge(sm["ex_done"], b - 1)
                    V.tensor_tensor(gap[b % 2][:, :], top[b % 2][:, :, 1], top[b % 2][:, :, 0], ALU.subtract
                                    ).then_inc(sm["gap_done"], 1)
                    dve.wait_ge(sm["topi_done"], NT * b + NT)
                    V.tensor_copy(topf[:, :, :], topi[:, :, 0:TOPK]).then_inc(sm["topf_done"], 1)
                    dve.wait_ge(sm["topf_done"], b + 1)
                    V.tensor_tensor(onehot[:, :, :, :].rearrange("p t k e -> p (t k) e"),
                                    topf[:, :, :].rearrange("p t k -> p (t k)").unsqueeze(2).to_broadcast([P, NT * TOPK, E]),
                                    const[:, C_IOTA8:C_IOTA8 + E].unsqueeze(1).to_broadcast([P, NT * TOPK, E]),
                                    ALU.is_equal).then_inc(sm["onehot_done"], 1)
                    dve.wait_ge(sm["onehot_done"], b + 1)
                    if b >= 2:
                        dve.wait_ge(sm["t_ps"], b - 1)
                    V.tensor_tensor(member[b % 2][:, :, :], onehot[:, :, 0, :], onehot[:, :, 1, :], ALU.add
                                    ).then_inc(sm["member_done"], 1)

            straight_steps(front, B, FRONT)

            dve.wait_ge(sm["base_done"], B)
            V.tensor_copy(fill_at[:, :], base[0:1, :]).then_inc(sm["plan_done"], 1)
            V.tensor_tensor(cnt[:, :], base[0:1, :], const[0:1, C_BASE:C_BASE + E], ALU.subtract
                            ).then_inc(sm["cnt_done"], 1)
            dve.wait_ge(sm["cnt_done"], 1)
            V.tensor_scalar(cnt_i[:, :], cnt[:, :], float(P - 1), None, ALU.add).then_inc(sm["cnti_done"], 1)
            dve.wait_ge(sm["cnti_done"], 1)
            V.tensor_single_scalar(til_i[:, :], cnt_i[:, :], P.bit_length() - 1, op=ALU.arith_shift_right
                                   ).then_inc(sm["tili_done"], 1)
            dve.wait_ge(sm["tili_done"], 1)
            V.tensor_copy(til[:, :], til_i[:, :]).then_inc(sm["til_done"], 1)
            dve.wait_ge(sm["til_done"], 1)
            V.tensor_tensor(cumm[:, :, :], til[:, :].unsqueeze(1).to_broadcast([1, E, E]),
                            const[0:1, C_CUM:C_CUM + E * E].rearrange("p (a b) -> p a b", a=E), ALU.mult
                            ).then_inc(sm["cumm_done"], 1)
            dve.wait_ge(sm["cumm_done"], 1)
            V.tensor_reduce(cum[:, :], cumm[:, :, :], AX.X, ALU.add).then_inc(sm["cum_done"], 1)
            dve.wait_ge(sm["cum_done"], 1)
            V.tensor_tensor(done[:, :, :], cum[:, :].unsqueeze(1).to_broadcast([1, MOE_TILES, E]),
                            const[0:1, C_TILE:C_TILE + MOE_TILES].unsqueeze(2).to_broadcast([1, MOE_TILES, E]),
                            ALU.is_le).then_inc(sm["dn_done"], 1)
            dve.wait_ge(sm["dn_done"], 1)
            V.tensor_tensor(donet[:, :, :], done[:, :, :], til[:, :].unsqueeze(1).to_broadcast([1, MOE_TILES, E]),
                            ALU.mult).then_inc(sm["dnt_done"], 1)
            V.tensor_reduce(eidx[:, :], done[:, :, :], AX.X, ALU.add).then_inc(sm["eidx_done"], 1)
            dve.wait_ge(sm["dnt_done"], 1)
            V.tensor_reduce(past[:, :], donet[:, :, :], AX.X, ALU.add).then_inc(sm["past_done"], 1)
            dve.wait_ge(sm["eidx_done"], 1)
            V.tensor_scalar(woff[:, :], eidx[:, :], float(E - 1), float(INTER), ALU.min, ALU.mult
                            ).then_inc(sm["plan_done"], 1)
            V.tensor_scalar(ereg[:, :], eidx[:, :], float(REGION), None, ALU.mult).then_inc(sm["ereg_done"], 1)
            dve.wait_ge(sm["past_done"], 1)
            V.tensor_tensor(row_f[:, :], const[0:1, C_TILE:C_TILE + MOE_TILES], past[:, :], ALU.subtract
                            ).then_inc(sm["row_done"], 1)
            dve.wait_ge(sm["row_done"], 1)
            dve.wait_ge(sm["ereg_done"], 1)
            V.scalar_tensor_tensor(ereg[:, :], row_f[:, :], float(P), ereg[:, :], ALU.mult, ALU.add
                                   ).then_inc(sm["ereg_done"], 1)
            dve.wait_ge(sm["ereg_done"], 2)
            V.tensor_scalar(rowoff[:, :], ereg[:, :], float(PAD_ROW), None, ALU.min).then_inc(sm["plan_done"], 1)

            def experts(s, r, live):
                if live(0):
                    dve.wait_ge(sm["t32_done"], s + 1)
                    if far(s, 2):
                        dve.wait_ge(sm["u_ps"], s - 1)
                    V.tensor_copy(t_hi[r % 2][:, :], t32[r % 2][:, :]).then_inc(sm["thi_done"], 1)
                    dve.wait_ge(sm["thi_done"], s + 1)
                    V.tensor_tensor(t_lo[r % 2][:, :], t32[r % 2][:, :], t_hi[r % 2][:, :].bitcast(F32), ALU.subtract
                                    ).then_inc(sm["tlo_done"], 1)
                if live(1):
                    i, i2, r1 = s - 1, (r - 1) % 2, (r - 1) % RING
                    dve.wait_ge(sm["sg_done"], i + 1)
                    dve.wait_ge(sm["u_ps"], i + 1)
                    if far(i, 2):
                        dve.wait_ge(sm["hT_ps"], i - 1)
                    V.scalar_tensor_tensor(hid[i2][:, :], sg[i2][:, :], xrow[r1][:, D:D + 1], banks[2 + i2][:, :],
                                           ALU.mult, ALU.mult).then_inc(sm["hid_done"], 1)
                if live(2):
                    i, i2 = s - 2, r % 2
                    dve.wait_ge(sm["hT_ps"], i + 1)
                    if far(i, 2):
                        dve.wait_ge(sm["y_ps"], i - 1)
                    V.tensor_copy(hidT[i2][:, :], banks[4 + i2][:, :]).then_inc(sm["hT_sb"], 1)

            looped_steps(dve, experts, MOE_TILES, 3)

            def finish(s, live):
                if live(0):
                    dve.wait_ge(sm["z0_done"], s + 1)
                    V.tensor_tensor(x1_all[:, s, :, :], x1_all[:, s, :, :], yin[s % RING][:, :, 1, :], ALU.add
                                    ).then_inc(sm["z_done"], 1)
                    dve.wait_ge(sm["z_done"], s + 1)
                    for t in range(NT):
                        V.bn_stats(st3[:, t, :], x1_all[:, s, t, :]).then_inc(sm["st3_done"], 1)
                    for t in range(NT):
                        dve.wait_ge(sm["st3_done"], NT * s + t + 1)
                        if s >= 2:
                            dve.wait_ge(sm["shift3_done"], s - 1)
                        V.bn_aggr(mv3[s % 2][:, t, :], st3[:, t, :]).then_inc(sm["mv3_done"], 1)
                    dve.wait_ge(sm["mv3_done"], NT * s + NT)
                    if s >= 2:
                        dve.wait_ge(sm["rs3_done"], s - 1)
                    V.tensor_scalar(var3[s % 2][:, :], mv3[s % 2][:, :, 1], EPS, None, ALU.add).then_inc(sm["var3_done"], 1)
                if live(1):
                    b = s - 1
                    dve.wait_ge(sm["rs3_done"], b + 1)
                    if b >= 2:
                        dve.wait_ge(sm["o_done"], NT * (b - 1))
                    V.scalar_tensor_tensor(shift3[b % 2][:, :], mv3[b % 2][:, :, 0], -1.0, rs3[b % 2][:, :],
                                           ALU.mult, ALU.mult).then_inc(sm["shift3_done"], 1)

            straight_steps(finish, B, 1)

        @block.gpsimd
        def _(pool):
            G = nc.gpsimd
            G.memset(zero_i[:, :], 0).then_inc(sm["zero_ready"], 1)
            pool.wait_ge(sm["half_ready"], 1)

            def send(b):
                if not 0 <= b < B:
                    return
                pool.wait_ge(sm["place_done"], b + 1)
                pool.wait_ge(sm["meta_done"], 2 * b + 2)
                pool.wait_ge(sm["n2_done"], NT * b + NT)
                for t in range(NT):
                    for k in range(TOPK):
                        G.indirect_dma_start(
                            out=expert_rows[:, :],
                            out_offset=bass.IndirectOffsetOnAxis(ap=place[b % NR][:, t, k:k + 1], axis=0),
                            in_=rows[b % NR][:, t, k, :], in_offset=None).then_inc(sent[b % NR], 16)

            def front(s, live):
                if s >= B+4:
                    send(s - 6)
                if live(3):
                    b = s - 3
                    pool.wait_ge(sm["var0_done"], 2 * b + 2)
                    if b >= 2:
                        pool.wait_ge(sm["x1_done"], NT * (b - 1))
                        pool.wait_ge(sm["n1_done"], NT * (b - 1))
                    G.tensor_tensor(rs0[b % 2][:, :, :].rearrange("p a t -> p (a t)"),
                                    var0[b % 2][:, :, :].rearrange("p a t -> p (a t)"), mhalf[:, :], ALU.pow
                                    ).then_inc(sm["rs0_done"], 1)
                if live(4):
                    b = s - 4
                    pool.wait_ge(sm["var2_done"], b + 1)
                    if b >= 2:
                        pool.wait_ge(sm["n2_done"], NT * (b - 1))
                    G.tensor_tensor(rs2[b % 2][:, :], var2[b % 2][:, :], mhalf[:, 0:NT], ALU.pow
                                    ).then_inc(sm["rs2_done"], 1)
                if s < B+4:
                    send(s - 6)

            straight_steps(front, B, FRONT)

            pool.wait_ge(sm["h_done"], B)
            pool.wait_ge(sm["x1_done"], NT * B)
            whole = lambda a: a[:, :, :, :].rearrange("p b t d -> p (b t d)")
            G.tensor_tensor(whole(x1_all), whole(x1_all), whole(h_all), ALU.add).then_inc(sm["res_done"], 1)

            last_row = pool.to_reg(Y_ROWS - 1)

            def experts(s, r, live):
                if live(3):
                    pool.wait_ge(sm["idx_done"], s - 2)
                    pool.wait_ge(sm["ysb_done"], s - 2)
                if live(1):
                    i, r1 = s - 1, (r - 1) % RING
                    pool.wait_ge(xr_in[r1], turn(i, r1))
                    if far(i, RING):
                        pool.wait_ge(y_sent[r1], turn(i, r1) - 16)
                    G.tensor_tensor(idx[r1][:, :], xrow[r1][:, D + 1:D + 2].bitcast(I32), zero_i[:, :], ALU.add
                                    ).then_inc(sm["idx_done"], 1)
                if live(3):
                    r3 = (r - 3) % RING
                    G.indirect_dma_start(
                        out=moe_rows[:, :], out_offset=bass.IndirectOffsetOnAxis(ap=idx[r3][:, :], axis=0),
                        in_=ysb[r3][:, :], in_offset=None, bounds_check=last_row, oob_is_err=False
                    ).then_inc(y_sent[r3], 16)

            looped_steps(pool, experts, MOE_TILES, 3)

            pool.wait_ge(sm["res_done"], 1)

            def finish(s, live):
                if live(0):
                    pool.wait_ge(y_in[s % RING], turn(s, s % RING))
                    G.tensor_tensor(x1_all[:, s, :, :], x1_all[:, s, :, :], yin[s % RING][:, :, 0, :], ALU.add
                                    ).then_inc(sm["z0_done"], 1)
                if live(1):
                    b = s - 1
                    pool.wait_ge(sm["var3_done"], b + 1)
                    if b >= 2:
                        pool.wait_ge(sm["o_done"], NT * (b - 1))
                    G.tensor_tensor(rs3[b % 2][:, :], var3[b % 2][:, :], mhalf[:, 0:NT], ALU.pow
                                    ).then_inc(sm["rs3_done"], 1)

            straight_steps(finish, B, 1)


def kernel(**inputs):
    import concourse.bacc as bacc
    from concourse.bass_utils import run_bass_kernel_spmd

    a = {n[3:]: np.asarray(v) for n, v in inputs.items()}
    wqkv, bqkv = a["attn_W_qkv"], a["attn_b_qkv"]
    cols = [bqkv[0:D], bqkv[D:2 * D], bqkv[2 * D:], a["ffn_ln1_g"], a["ffn_ln1_b"], a["ffn_ln2_g"], a["ffn_ln2_b"]]
    par = np.concatenate([wqkv[:, 0:2 * D], wqkv[:, 2 * D:].T, a["attn_W_out"], a["ffn_attn_w"].T,
                          a["ffn_gate_w"].T, np.broadcast_to(a["attn_b_out"], (P, D)),
                          np.stack(cols, axis=1)], axis=1)
    arrays = {
        "x": np.ascontiguousarray(a["attn_x"]),
        "par": np.ascontiguousarray(par),
        "con": constants(),
        "dst": destinations(),
        "weights": np.ascontiguousarray(np.concatenate([
            a["ffn_gate_proj"].reshape(E * INTER, D).T, a["ffn_up_proj"].reshape(E * INTER, D).T,
            a["ffn_down_proj"].reshape(E, D, NC, P).transpose(3, 0, 2, 1).reshape(P, E * INTER)], axis=1)),
    }
    nc = bacc.Bacc("TRN2", target_bir_lowering=False, num_devices=1)
    aps = {n: nc.dram_tensor(n, v.shape, mybir.dt.from_np(v.dtype), kind="ExternalInput").ap()
           for n, v in arrays.items()}
    out = nc.dram_tensor("out", (B, S, D), F32, kind="ExternalOutput").ap()
    block_kernel(nc, out=out, **aps)
    r = run_bass_kernel_spmd(nc, [arrays], core_ids=[0])
    return r.results[0]["out"]
```
